# Optimizing a Trainium2 kernel written in Bass

```python
import numpy as np
import jax
import jax.numpy as jnp

def _softmax(x, axis=-1):
    return jax.nn.softmax(x, axis=axis)

def _gelu(x):
    return jax.nn.gelu(x, approximate=True)

def _silu(x):
    return jax.nn.silu(x)

def _sigmoid(x):
    return jax.nn.sigmoid(x)

def _layernorm(x, axis=-1, eps=1e-05):
    m = jnp.mean(x, axis=axis, keepdims=True)
    v = jnp.var(x, axis=axis, keepdims=True)
    return (x - m) / jnp.sqrt(v + eps)

def _scatter_add(tgt, idx, src, axis=0):
    return tgt.at[idx].add(src)

def _segment_sum(src, seg, n):
    return jax.ops.segment_sum(src, seg, n)
kernel_name = 'mk_xattn_ffn_d1_seqx_r4_e05991'

def setup_inputs(seed: int=0):
    np.random.seed(seed)
    _w = jnp.asarray

    def _rec_inputs():
        import jax
        import jax.numpy as jnp
        _rk = jax.random.key(seed)
        x = 7.22e-05 + 1 * jax.random.normal(jax.random.fold_in(_rk, 1), (4, 1024, 256), jnp.float32)
        _lenS = 1024 - jax.random.randint(jax.random.fold_in(_rk, 7), (4,), 0, max(1, 1024 // 4) + 1, jnp.int32)
        _lenS2 = 77 - jax.random.randint(jax.random.fold_in(_rk, 8), (4,), 0, max(1, 77 // 4) + 1, jnp.int32)
        _ctx_1024P = jax.random.normal(jax.random.fold_in(_rk, 11), (4, 16, 256), jnp.float32)
        _ctx_1024c = jax.random.dirichlet(jax.random.fold_in(_rk, 511), 0.3 * jnp.ones((16,), jnp.float32), (4, 77))
        _ctx_1024t = jnp.einsum('bsk,bkd->bsd', _ctx_1024c, _ctx_1024P)
        _ctx_1024t = _ctx_1024t * jax.lax.rsqrt(jnp.mean(jnp.square(_ctx_1024t)) + 1e-12) * 0.953939
        ctx_1024 = 4.13588e-05 + 0.999923 * (_ctx_1024t + 0.3 * jax.random.normal(jax.random.fold_in(_rk, 611), (4, 77, 256), jnp.float32))
        _validS = jnp.arange(1024)[None, :] < _lenS[:, None]
        _validS2 = jnp.arange(77)[None, :] < _lenS2[:, None]
        _causal = jnp.tril(jnp.ones((1024, 1024), dtype=bool))
        mask_Bx1xSxS2_bk1 = jnp.broadcast_to(_validS2[:, None, None, :], (4, 1, 1024, 77))
        return (x, ctx_1024, mask_Bx1xSxS2_bk1)
    x, ctx_1024, mask_Bx1xSxS2_bk1 = _rec_inputs()

    def _L0_xattn_setup():
        import jax, jax.numpy as jnp
        import numpy as np
        B, S, D, H = (4, 512, 256, 16)
        HD = D // H

        def _split_heads(x):
            b, s, _ = x.shape
            return x.reshape(b, s, H, HD).transpose(0, 2, 1, 3)
        key = jax.random.key(seed)
        ks = jax.random.split(key, 11)
        sc = 1.0 / np.sqrt(D)
        inp = {'q': jax.random.normal(ks[0], (B, S, D), jnp.float32), 'k': jax.random.normal(ks[1], (B, S, D), jnp.float32), 'v': jax.random.normal(ks[2], (B, S, D), jnp.float32), 'mask': jnp.broadcast_to(jnp.triu(jnp.ones((S, S), bool), k=1), (B, 1, S, S)), 'wq': jax.random.normal(ks[3], (D, D), jnp.float32) * sc, 'bq': jnp.zeros((D,), jnp.float32), 'wk': jax.random.normal(ks[4], (D, D), jnp.float32) * sc, 'bk': jnp.zeros((D,), jnp.float32), 'wv': jax.random.normal(ks[5], (D, D), jnp.float32) * sc, 'bv': jnp.zeros((D,), jnp.float32), 'wo': jax.random.normal(ks[6], (D, D), jnp.float32) * sc, 'bo': jnp.zeros((D,), jnp.float32)}
        return inp
    _L0_xattn_all = _L0_xattn_setup()
    _L0_xattn_in = {k: v for k, v in _L0_xattn_all.items() if k in ('wq', 'bq', 'wk', 'bk', 'wv', 'bv', 'wo', 'bo')}
    del _L0_xattn_all

    def _L0_ffn_setup():
        import jax, jax.numpy as jnp
        import numpy as np
        TOP_K = 2
        NUM_EXPERTS = 8
        key = jax.random.key(seed)
        ks = jax.random.split(key, 8)
        h, d, ds, E = (256, 128, 256, NUM_EXPERTS)
        s = 1.0 / np.sqrt(h)
        return {'x': jax.random.normal(ks[0], (2, 512, h), jnp.float32), 'router': jax.random.normal(ks[1], (h, E), jnp.float32) * s, 'experts_gate': jax.random.normal(ks[2], (E, h, d), jnp.float32) * s, 'experts_up': jax.random.normal(ks[3], (E, h, d), jnp.float32) * s, 'experts_down': jax.random.normal(ks[4], (E, d, h), jnp.float32) * (1.0 / np.sqrt(d)), 'shared_gate': jax.random.normal(ks[5], (h, ds), jnp.float32) * s, 'shared_up': jax.random.normal(ks[6], (h, ds), jnp.float32) * s, 'shared_down': jax.random.normal(ks[7], (ds, h), jnp.float32) * (1.0 / np.sqrt(ds))}
    _L0_ffn_all = _L0_ffn_setup()
    _L0_ffn_in = {k: v for k, v in _L0_ffn_all.items() if k in ('router', 'experts_gate', 'experts_up', 'experts_down', 'shared_gate', 'shared_up', 'shared_down')}
    del _L0_ffn_all
    return {'x': x, 'ctx_1024': ctx_1024, 'mask_Bx1xSxS2_bk1': mask_Bx1xSxS2_bk1, 'L0_xattn_wq': _L0_xattn_in['wq'], 'L0_xattn_bq': _L0_xattn_in['bq'], 'L0_xattn_wk': _L0_xattn_in['wk'], 'L0_xattn_bk': _L0_xattn_in['bk'], 'L0_xattn_wv': _L0_xattn_in['wv'], 'L0_xattn_bv': _L0_xattn_in['bv'], 'L0_xattn_wo': _L0_xattn_in['wo'], 'L0_xattn_bo': _L0_xattn_in['bo'], 'L0_ffn_router': _L0_ffn_in['router'], 'L0_ffn_experts_gate': _L0_ffn_in['experts_gate'], 'L0_ffn_experts_up': _L0_ffn_in['experts_up'], 'L0_ffn_experts_down': _L0_ffn_in['experts_down'], 'L0_ffn_shared_gate': _L0_ffn_in['shared_gate'], 'L0_ffn_shared_up': _L0_ffn_in['shared_up'], 'L0_ffn_shared_down': _L0_ffn_in['shared_down']}

def reference(x, ctx_1024, mask_Bx1xSxS2_bk1, L0_xattn_wq, L0_xattn_bq, L0_xattn_wk, L0_xattn_bk, L0_xattn_wv, L0_xattn_bv, L0_xattn_wo, L0_xattn_bo, L0_ffn_router, L0_ffn_experts_gate, L0_ffn_experts_up, L0_ffn_experts_down, L0_ffn_shared_gate, L0_ffn_shared_up, L0_ffn_shared_down):
    import jax
    import jax.numpy as jnp

    def _L0_xattn_ref(q, k, v, mask, wq, bq, wk, bk, wv, bv, wo, bo):
        import jax, jax.numpy as jnp
        import numpy as np
        B, S, D, H = (4, 512, 256, 16)
        HD = D // H

        def _split_heads(x):
            b, s, _ = x.shape
            return x.reshape(b, s, H, HD).transpose(0, 2, 1, 3)
        qh = _split_heads(q @ wq + bq)
        kh = _split_heads(k @ wk + bk)
        vh = _split_heads(v @ wv + bv)
        scale = 1.0 / jnp.sqrt(jnp.asarray(HD, jnp.float32))
        scores = jnp.einsum('bhsd,bhtd->bhst', qh, kh) * scale
        scores = jnp.where(mask, -jnp.inf, scores)
        attn = jax.nn.softmax(scores, axis=-1)
        out = jnp.einsum('bhst,bhtd->bhsd', attn, vh)
        out = out.transpose(0, 2, 1, 3).reshape(q.shape[0], q.shape[1], D)
        return out @ wo + bo

    def _L0_ffn_ref(x, router, experts_gate, experts_up, experts_down, shared_gate, shared_up, shared_down):
        import jax, jax.numpy as jnp
        import numpy as np
        TOP_K = 2
        NUM_EXPERTS = 8
        b, s, h = x.shape
        E = router.shape[1]
        shared_act = jax.nn.silu(jnp.einsum('bsh,hd->bsd', x, shared_gate))
        shared_up_out = jnp.einsum('bsh,hd->bsd', x, shared_up)
        shared_out = jnp.einsum('bsd,dh->bsh', shared_act * shared_up_out, shared_down)
        router_probs = jax.nn.softmax(jnp.einsum('bsh,he->bse', x, router), axis=-1)
        topk_probs, topk_idx = jax.lax.top_k(router_probs, TOP_K)
        coef = jnp.sum(jax.nn.one_hot(topk_idx, E, dtype=x.dtype) * topk_probs[..., None], axis=2)
        coef = coef.reshape(b * s, E)
        x_flat = x.reshape(b * s, h)
        gate = jnp.einsum('th,ehd->etd', x_flat, experts_gate)
        up = jnp.einsum('th,ehd->etd', x_flat, experts_up)
        expert_out = jnp.einsum('etd,edh->eth', jax.nn.silu(gate) * up, experts_down)
        routed = jnp.einsum('eth,te->th', expert_out, coef)
        return routed.reshape(b, s, h) + shared_out
    x = x + _L0_xattn_ref(_layernorm(x, axis=-1), ctx_1024, ctx_1024, mask_Bx1xSxS2_bk1, L0_xattn_wq, L0_xattn_bq, L0_xattn_wk, L0_xattn_bk, L0_xattn_wv, L0_xattn_bv, L0_xattn_wo, L0_xattn_bo)
    x = x + _L0_ffn_ref(_layernorm(x, axis=-1), L0_ffn_router, L0_ffn_experts_gate, L0_ffn_experts_up, L0_ffn_experts_down, L0_ffn_shared_gate, L0_ffn_shared_up, L0_ffn_shared_down)
    return x

_drawn_inputs = setup_inputs


def setup_inputs(seed=0):
    import zlib

    import numpy as np

    out = dict(_drawn_inputs(seed))
    spreads = {'L0_xattn_bq': (0.0, 0.1),
     'L0_xattn_bk': (0.0, 0.1),
     'L0_xattn_bv': (0.0, 0.1),
     'L0_xattn_bo': (0.0, 0.1)}
    factors = {}
    for name, (base, spread) in spreads.items():
        noise = np.random.default_rng([zlib.crc32(name.encode()), seed]).standard_normal(out[name].shape)
        drawn = base * np.exp(spread * noise) if base else spread * noise
        out[name] = jnp.asarray(drawn.astype(out[name].dtype))
    for name, factor in factors.items():
        out[name] = (out[name] * factor).astype(out[name].dtype)
    return out
```

```python
from contextlib import ExitStack

import numpy as np
import concourse.bass as bass
from concourse import mybir

F32 = mybir.dt.float32
F32R = mybir.dt.float32r
BF16 = mybir.dt.bfloat16
U8 = mybir.dt.uint8
ALU = mybir.AluOpType
ACT = mybir.ActivationFunctionType
AX = mybir.AxisListType

B, S, D = 4, 1024, 256
KEYS, HEADS, HD = 77, 16, 16
E, DE, DS = 8, 128, 256
P = 128
C = D // P
HC = HEADS // C
GT = 512
TG = GT // P
NG = B * S // GT
NT = B * S // P
HK = HC * KEYS
NJ = (HK + P - 1) // P
VW = HD + 1
MASKED = -(2.0 ** 120)
EPS = 1e-5
MROW = 96
HC_UNIT = 6
UNITS = [(0, 6), (6, 12), (12, 16)]
TILE_HEADS = [(P * j // KEYS, min(P * (j + 1) - 1, HK - 1) // KEYS - P * j // KEYS + 1) for j in range(NJ)]
NHMAX = max(n for _, n in TILE_HEADS)


def constants():
    f = np.arange(NJ * P)
    head, key = f // KEYS, f % KEYS
    live = f < HK
    sel = np.zeros((P, C, NJ * P), np.float32)
    for c in range(C):
        sel[key[live], c, f[live]] = 1.0
        sel[MROW + head[live] + c * HC, c, f[live]] = -1.0
        sel[MROW + HEADS + head[live] + c * HC, c, f[live]] = -1.0
    vmask = np.zeros((P, NJ, NHMAX, VW), np.float32)
    for j, (h0, n) in enumerate(TILE_HEADS):
        for h in range(n):
            rows = f[(f // P == j) & live & (head == h0 + h)]
            vmask[rows % P, j, h, :] = 1.0
    ksel = np.zeros((P, HC), np.float32)
    ksel[np.arange(P), np.arange(P) // HD] = 1.0 / np.sqrt(HD)
    return {"c_sel": sel.reshape(P, -1), "c_vmask": vmask.reshape(P, -1), "c_ksel": ksel,
            "c_ident": np.eye(P, dtype=np.float32)}


def build(nc, a, out, kscr):
    with nc.sbuf_tensor("x_res", [P, NT, D], F32) as x_res, nc.sbuf_tensor("ident", [P, P], F32) as ident:
        attention(nc, a, kscr, x_res, ident)
        feed_forward(nc, a, out, x_res, ident)


def attention(nc, a, kscr, x_res, ident):
    ctx = ExitStack()
    with ctx:
        def sb(name, shape, dt=F32):
            return ctx.enter_context(nc.sbuf_tensor(name, shape, dt))

        def ps(name, shape, dt=F32):
            return ctx.enter_context(nc.psum_tensor(name, shape, dt))

        def sem(name):
            return ctx.enter_context(nc.semaphore(name))

        def f32(ap):
            return ap.bitcast(F32)

        ident_r = sb("ident_r", [P, P], F32R)
        ident_b = sb("ident_b", [P, P], BF16)
        sel_raw = sb("sel_raw", [P, C * NJ * P])
        sel_r = sb("sel_r", [P, C, NJ * P], F32R)
        vmask = sb("vmask", [P, NJ, NHMAX, VW])
        ksel = sb("ksel", [P, HC])
        w_raw = sb("w_raw", [P, 4, C, D])
        w_hi = sb("w_hi", [P, 2, C, D], F32R)
        w_lo = sb("w_lo", [P, 2, C, D], F32R)
        bq = sb("bq", [P, C])
        bk = sb("bk", [P, C])
        bv = sb("bv", [1, D])
        bo = sb("bo", [P, D])
        ones1 = sb("ones1", [1, P])
        ctx_t = sb("ctx_t", [P, C, B * KEYS])
        kt = sb("kt", [P, C, B, KEYS])
        v_sb = sb("v_sb", [KEYS, B, D + HD])
        kb = sb("kb", [P, C, HC, KEYS])
        kb_hi = sb("kb_hi", [P, C, HK], F32R)
        kb_lo = sb("kb_lo", [P, C, HK], F32R)
        vb = sb("vb", [P, B, C, NJ, NHMAX, VW])
        kcur = sb("kcur", [P, 2, C, HK], F32R)
        kmax = sb("kmax", [P, C, HK], F32R)
        mk_raw = sb("mk_raw", [P, NG, TG * KEYS], U8)
        mt_raw = sb("mt_raw", [KEYS, NG, GT], U8)
        hold = sb("hold", [P, 1])
        mbias = sb("mbias", [P, 2, TG, KEYS], BF16)
        rhs_mm = sb("rhs_mm", [P, 2, GT], F32R)
        stats = sb("stats", [P, TG, 6])
        mv = sb("mv", [P, TG, 2])
        ve = sb("ve", [P, TG])
        rstd = sb("rstd", [P, TG])
        pow_e = sb("pow_e", [P, TG])
        xn = sb("xn", [P, TG, D])
        xn_hi = sb("xn_hi", [P, TG, D], F32R)
        xn_lo = sb("xn_lo", [P, TG, D], F32R)
        xnt = sb("xnt", [P, TG, 2 * C, P], F32R)
        q_hi = sb("q_hi", [P, 2, C, GT], F32R)
        q_lo = sb("q_lo", [P, 2, C, GT], F32R)
        mx = sb("mx", [P, TG, HEADS])
        mm = sb("mm", [P, TG, P], F32R)
        pt = sb("pt", [P, C * NJ, GT])
        allmasked = sb("allmasked", [P, TG, HEADS])
        nanfix = sb("nanfix", [P, 2, TG, HEADS])
        den = sb("den", [P, TG, HEADS])
        rden = sb("rden", [P, TG, HEADS])
        o = sb("o", [P, TG, D])
        o_hi = sb("o_hi", [P, TG, D], F32R)
        o_lo = sb("o_lo", [P, TG, D], F32R)
        ot = sb("ot", [P, TG, 2 * C, P], F32R)

        ps_mx = [ps(f"ps_mx{i}", [P, 512]) for i in range(2)]
        ps_sc = [ps(f"ps_sc{i}", [P, GT]) for i in range(2)]
        ps_t = [ps(f"ps_t{i}", [P, 2 * C, P]) for i in range(2)]
        ps_q = ps("ps_q", [P, 512])
        ps_pv = ps("ps_pv", [P, 512])

        const_in = sem("const_in")
        wattn_in = sem("wattn_in")
        x_in = sem("x_in")
        mask_in = sem("mask_in")
        consts_ready = sem("consts_ready")
        w_hi_ready = sem("w_hi_ready")
        w_lo_ready = sem("w_lo_ready")
        zeroed = sem("zeroed")
        prep_mm = sem("prep_mm")
        kt_ready = sem("kt_ready")
        v_ready = sem("v_ready")
        kb_raw_done = sem("kb_raw_done")
        kb_hi_done = sem("kb_hi_done")
        kb_lo_done = sem("kb_lo_done")
        kb_stored = sem("kb_stored")
        vb_mm = sem("vb_mm")
        vb_done = sem("vb_done")
        kmax_in = sem("kmax_in")
        kcur_in = sem("kcur_in")
        nan_step = sem("nan_step")
        stat_step = sem("stat_step")
        aggr_step = sem("aggr_step")
        mx_hi_step = sem("mx_hi_step")
        den_step = sem("den_step")
        rden_step = sem("rden_step")
        prep_act = sem("prep_act")
        mask_ready = sem("mask_ready")
        stats_ready = sem("stats_ready")
        rstd_ready = sem("rstd_ready")
        xn_ready = sem("xn_ready")
        xn_hi_ready = sem("xn_hi_ready")
        xn_lo_ready = sem("xn_lo_ready")
        xb_ready = sem("xb_ready")
        xnt_filled = sem("xnt_filled")
        xnt_act = sem("xnt_act")
        xnt_dve = sem("xnt_dve")
        q_filled = sem("q_filled")
        q_hi_ready = sem("q_hi_ready")
        q_lo_ready = sem("q_lo_ready")
        mx_filled = sem("mx_filled")
        mx_used = sem("mx_used")
        mm_ready = sem("mm_ready")
        mt_filled = sem("mt_filled")
        mt_ready = sem("mt_ready")
        nan_ready = sem("nan_ready")
        sc_filled = sem("sc_filled")
        exp_done = sem("exp_done")
        pv_filled = sem("pv_filled")
        o_ready = sem("o_ready")
        o_hi_ready = sem("o_hi_ready")
        o_lo_ready = sem("o_lo_ready")
        ot_filled = sem("ot_filled")
        ot_act = sem("ot_act")
        ot_dve = sem("ot_dve")
        op_filled = sem("op_filled")
        x1_ready = sem("x1_ready")

        x_v = a["x"].rearrange("b (g p i) d -> (b g) p i d", p=P, i=TG)
        mk_v = a["mask_tok"]
        mt_v = a["mask_key"]
        Q, K, V, O = range(4)

        NCONST = 16 * 4
        NATTN = 16 * (4 + 4 + 1)

        block = ctx.enter_context(nc.Block())

        @block.sync
        def _(sp):
            def load_x(g):
                if g:
                    sp.wait_ge(x_in, 16 * g)
                sp.dma_start(x_res[:, g * TG:(g + 1) * TG, :], x_v[g]).then_inc(x_in, 16)

            load_x(0)
            sp.dma_start(mk_raw[:], mk_v.rearrange("g p k -> p g k")).then_inc(mask_in, 16)
            sp.dma_start(mt_raw[:], mt_v.rearrange("g k t -> k g t")).then_inc(mask_in, 16)
            sp.dma_start(ident[:], a["c_ident"]).then_inc(const_in, 16)
            for i, name in enumerate(("wq", "wk", "wv", "wo")):
                sp.dma_start(w_raw[:, i], a[name].rearrange("(c p) n -> p c n", p=P)).then_inc(wattn_in, 16)
            sp.dma_start(ctx_t[:], a["ctx_t"].rearrange("(c p) n -> p c n", p=P)).then_inc(wattn_in, 16)
            sp.dma_start(bq[:], a["bq"]).then_inc(wattn_in, 16)
            sp.dma_start(bk[:], a["bk"]).then_inc(wattn_in, 16)
            sp.dma_start(bv[:], a["bv"]).then_inc(wattn_in, 16)
            sp.dma_start(bo[:], a["bo"].to_broadcast([P, D])).then_inc(wattn_in, 16)
            sp.dma_start(sel_raw[:], a["c_sel"]).then_inc(const_in, 16)
            sp.dma_start(vmask[:].rearrange("p j h v -> p (j h v)"), a["c_vmask"]).then_inc(const_in, 16)
            sp.dma_start(ksel[:], a["c_ksel"]).then_inc(const_in, 16)
            for g in range(1, NG):
                load_x(g)
            for b in range(B):
                sp.wait_ge(kb_hi_done, b + 1)
                sp.dma_start(kscr[b, 0], f32(kb_hi[:])).then_inc(kb_stored, 16)
                sp.wait_ge(kb_lo_done, b + 1)
                sp.dma_start(kscr[b, 1], f32(kb_lo[:])).then_inc(kb_stored, 16)
                sp.wait_ge(kb_stored, 32 * (b + 1))
            sp.dma_start(f32(kmax[:]), kscr[0, 0]).then_inc(kmax_in, 16)

            def keys_for_scores(b):
                sp.dma_start(f32(kcur[:]), kscr[bass.ds(b, 1)].rearrange("o h p c n -> p (o h) c n")).then_inc(kcur_in, 16)

            def keys_for_maxima(b):
                sp.dma_start(f32(kmax[:]), kscr[bass.ds(b, 1), 0].rearrange("o p c n -> p (o c) n")).then_inc(kmax_in, 16)

            sp.dma_start(f32(kcur[:]), kscr[0].rearrange("h p c n -> p h c n")).then_inc(kcur_in, 16)
            with sp.Fori(0, NG - 3, 2) as r:
                sp.wait_ge(mx_filled, 3 * TG * (r + 2))
                keys_for_maxima(r // 2 + 1)
                sp.wait_ge(sc_filled, C * NJ * (r + 2))
                keys_for_scores(r // 2 + 1)

        @block.gpsimd
        def _(pool):
            g_ = nc.gpsimd
            g_.memset(ones1[:], 1.0).then_inc(zeroed, 1)
            g_.memset(f32(mm[:]), 0.0).then_inc(zeroed, 1)
            g_.memset(pow_e[:], -0.5).then_inc(zeroed, 1)
            g_.memset(v_sb[:, :, D:], 0.0).then_inc(zeroed, 1)
            pool.wait_ge(zeroed, 5)
            pool.wait_ge(wattn_in, NATTN)

            def norm(g):
                pool.wait_ge(stats_ready, g + 1)
                g_.tensor_tensor(rstd[:], ve[:], pow_e[:], ALU.pow).then_inc(rstd_ready, 1)

            def low(g):
                pool.wait_ge(xn_hi_ready, g + 1)
                g_.tensor_tensor(xn_lo[:], xn[:], f32(xn_hi[:]), ALU.subtract).then_inc(xn_lo_ready, 1)
                for i in range(TG):
                    at = x_res[:, bass.ds(g * TG + i, 1), :].rearrange("p o d -> p (o d)")
                    g_.tensor_tensor(at, at, bo[:], ALU.add).then_inc(xb_ready, 1)

            def o_low(g):
                for t in range(TG):
                    pool.wait_ge(o_hi_ready, TG * g + t + 1)
                    g_.tensor_tensor(o_lo[:, t], o[:, t], f32(o_hi[:, t]), ALU.subtract).then_inc(o_lo_ready, 1)

            for g in range(2):
                norm(g)
                low(g)

            def step(g, u, scores_next, project_next):
                if project_next:
                    norm(g + 2)
                    low(g + 2)
                o_low(g)

            for g in range(2):
                step(g, g, True, True)
            with pool.Fori(2, NG - 3, 2) as r:
                for u in range(2):
                    step(r + u, u, True, True)
            step(NG - 2, 0, True, False)
            step(NG - 1, 1, False, False)

        @block.scalar
        def _(act):
            def copy(dst, src):
                return nc.scalar.activation(dst, src, ACT.Copy)

            act.wait_ge(const_in, NCONST)
            copy(ident_r[:], ident[:]).then_inc(consts_ready, 1)
            copy(ident_b[:], ident[:]).then_inc(consts_ready, 1)
            copy(sel_r[:].rearrange("p c n -> p (c n)"), sel_raw[:]).then_inc(consts_ready, 1)
            act.wait_ge(wattn_in, NATTN)
            copy(w_hi[:, 0], w_raw[:, Q]).then_inc(w_hi_ready, 1)
            copy(w_hi[:, 1], w_raw[:, O]).then_inc(w_hi_ready, 1)
            act.wait_ge(zeroed, 5)
            for b in range(B):
                act.wait_ge(prep_mm, C + b + 1)
                copy(v_sb[:, b, 0:D], ps_mx[b % 2][0:KEYS, 0:D]).then_inc(v_ready, 1)

            def normal_high(g):
                act.wait_ge(xn_ready, g + 1)
                act.wait_ge(xnt_filled, TG * g)
                copy(xn_hi[:], xn[:]).then_inc(xn_hi_ready, 1)

            def project(g, u):
                for i in (0, 2):
                    act.wait_ge(xnt_filled, TG * g + i + 1)
                    act.wait_ge(q_filled, C * g)
                    copy(xnt[:, i], ps_t[0][:]).then_inc(xnt_act, 1)
                for c in range(C):
                    act.wait_ge(q_filled, C * g + c + 1)
                    nc.scalar.activation(q_hi[:, u, c], ps_q[:], ACT.Identity, bias=bq[:, c:c + 1]).then_inc(q_hi_ready, 1)

            def exps(g, js):
                for j in js:
                    rows = min(P, HK - (j % NJ) * P)
                    act.wait_ge(sc_filled, C * NJ * g + j + 1)
                    act.wait_ge(pv_filled, TG * g)
                    nc.scalar.activation(pt[0:rows, j], ps_sc[j % 2][0:rows], ACT.Exp).then_inc(exp_done, 1)

            def heads_high(g):
                for t in range(TG):
                    act.wait_ge(o_ready, TG * g + t + 1)
                    copy(o_hi[:, t], o[:, t]).then_inc(o_hi_ready, 1)

            def heads_transposed(g):
                for t in (0, 2):
                    act.wait_ge(ot_filled, TG * g + t + 1)
                    copy(ot[:, t], ps_t[0][:]).then_inc(ot_act, 1)

            normal_high(0)
            project(0, 0)
            for b in range(B):
                act.wait_ge(kb_raw_done, b + 1)
                if b >= 1:
                    act.wait_ge(kb_stored, 32 * b)
                copy(kb_hi[:].rearrange("p c n -> p (c n)"), kb[:].rearrange("p c h k -> p (c h k)")).then_inc(kb_hi_done, 1)
            normal_high(1)
            project(1, 1)

            def step(g, u, scores_next, project_next):
                exps(g, range(0, 5))
                if project_next:
                    normal_high(g + 2)
                exps(g, range(5, C * NJ))
                heads_high(g)
                if project_next:
                    project(g + 2, u)
                heads_transposed(g)

            for g in range(2):
                step(g, g, True, True)
            with act.Fori(2, NG - 3, 2) as r:
                for u in range(2):
                    step(r + u, u, True, True)
            step(NG - 2, 0, True, False)
            step(NG - 1, 1, False, False)

        @block.vector
        def _(dve):
            v_ = nc.vector

            def masks(g, u):
                if not isinstance(g, int):
                    dve.wait_ge(sc_filled, C * NJ * (g - 1))
                v_.tensor_scalar(mbias[:, u].rearrange("p i k -> p (i k)"),
                                 mk_raw[:, bass.ds(g, 1)].rearrange("p o k -> p (o k)"),
                                 MASKED, None, ALU.mult).then_inc(mask_ready, 1)
                v_.tensor_scalar(rhs_mm[0:KEYS, u], mt_raw[:, bass.ds(g, 1)].rearrange("p o k -> p (o k)"),
                                 MASKED, None, ALU.mult).then_inc(mask_ready, 1)

            def nans(g, u):
                v_.tensor_scalar(allmasked[:], mx[:], MASKED / 2, 3e38, ALU.is_le, ALU.mult).then_inc(nan_step, 1)
                dve.wait_ge(nan_step, g + 1)
                v_.tensor_scalar(nanfix[:, u], allmasked[:], 3e38, 0.0, ALU.mult, ALU.mult).then_inc(nan_ready, 1)

            def stats_of(g):
                dve.wait_ge(x_in, (g + 1) * 16)
                for i in range(TG):
                    v_.bn_stats(stats[:, i], x_res[:, bass.ds(g * TG + i, 1), :].rearrange("p o d -> p (o d)")
                                ).then_inc(stat_step, 1)
                dve.wait_ge(stat_step, TG * (g + 1))
                v_.memset(hold[:], 0.0)
                for i in range(TG):
                    v_.bn_aggr(mv[:, i], stats[:, i]).then_inc(aggr_step, 1)
                dve.wait_ge(aggr_step, TG * (g + 1))
                v_.tensor_scalar(ve[:], mv[:, :, 1], EPS, None, ALU.add).then_inc(stats_ready, 1)

            def normalise(g):
                dve.wait_ge(rstd_ready, g + 1)
                dve.wait_ge(xn_lo_ready, g)
                for i in range(TG):
                    last = v_.tensor_scalar(xn[:, i], x_res[:, bass.ds(g * TG + i, 1), :].rearrange("p o d -> p (o d)"),
                                            mv[:, i, 0:1], rstd[:, i:i + 1], ALU.subtract, ALU.mult)
                last.then_inc(xn_ready, 1)

            def project(g, u):
                for i in (1, 3):
                    dve.wait_ge(xnt_filled, TG * g + i + 1)
                    dve.wait_ge(q_filled, C * g)
                    v_.tensor_copy(xnt[:, i], ps_t[1][:]).then_inc(xnt_dve, 1)
                for c in range(C):
                    dve.wait_ge(q_hi_ready, C * g + c + 1)
                    v_.scalar_tensor_tensor(q_lo[:, u, c], ps_q[:], bq[:, c:c + 1], f32(q_hi[:, u, c]), ALU.add,
                                            ALU.subtract).then_inc(q_lo_ready, 1)

            def maxima(g, units):
                for n in units:
                    i, k = n // 3, n % 3
                    h0, h1 = UNITS[k]
                    dve.wait_ge(mx_filled, 3 * TG * g + n + 1)
                    v_.tensor_reduce(mx[:, i, h0:h1],
                                     ps_mx[n % 2][:, 0:(h1 - h0) * KEYS].rearrange("p (h k) -> p h k", k=KEYS),
                                     AX.X, ALU.max).then_inc(mx_used, 1)

            def maxima_parts(g, u):
                dve.wait_ge(mx_used, 3 * TG * (g + 1))
                v_.tensor_copy(mm[:, :, MROW:MROW + HEADS], mx[:]).then_inc(mx_hi_step, 1)
                dve.wait_ge(mx_hi_step, g + 1)
                v_.tensor_tensor(mm[:, :, MROW + HEADS:], mx[:], f32(mm[:, :, MROW:MROW + HEADS]), ALU.subtract
                                 ).then_inc(mm_ready, 1)
                nans(g, u)
                dve.wait_ge(mt_filled, g + 1)
                v_.tensor_copy(rhs_mm[MROW:, u], ps_t[1][MROW:].rearrange("p i t -> p (i t)")).then_inc(mt_ready, 1)

            def heads(g, u):
                dve.wait_ge(nan_ready, g + 1)
                for t in range(TG):
                    num = ps_pv[:, 0:HEADS * VW].rearrange("p (h v) -> p h v", v=VW)
                    dve.wait_ge(pv_filled, TG * g + t + 1)
                    v_.tensor_tensor(den[:, t], num[:, :, HD], nanfix[:, u, t], ALU.add).then_inc(den_step, 1)
                    dve.wait_ge(den_step, TG * g + t + 1)
                    v_.reciprocal(rden[:, t], den[:, t]).then_inc(rden_step, 1)
                    dve.wait_ge(rden_step, TG * g + t + 1)
                    v_.tensor_tensor(o[:, t].rearrange("p (h d) -> p h d", d=HD), num[:, :, 0:HD],
                                     rden[:, t].unsqueeze(2).to_broadcast([P, HEADS, HD]), ALU.mult).then_inc(o_ready, 1)

            def residual(g, t):
                dve.wait_ge(op_filled, TG * g + t + 1)
                dve.wait_ge(xb_ready, TG * (g + 1))
                at = x_res[:, bass.ds(g * TG + t, 1), :].rearrange("p o d -> p (o d)")
                v_.tensor_tensor(at, ps_q[:, 0:D], at, ALU.add).then_inc(x1_ready, 1)

            def heads_transposed(g, t):
                dve.wait_ge(ot_filled, TG * g + t + 1)
                v_.tensor_copy(ot[:, t], ps_t[1][:]).then_inc(ot_dve, 1)

            v_.memset(f32(rhs_mm[64:P]), 0.0).then_inc(zeroed, 1)
            stats_of(0)
            normalise(0)
            for n, i in ((0, Q), (1, O)):
                dve.wait_ge(w_hi_ready, n + 1)
                v_.tensor_tensor(w_lo[:, n], w_raw[:, i], f32(w_hi[:, n]), ALU.subtract).then_inc(w_lo_ready, 1)
            for c in range(C):
                dve.wait_ge(prep_mm, c + 1)
                v_.tensor_scalar(kt[:, c].rearrange("p b k -> p (b k)"), ps_sc[c][:, 0:B * KEYS], bk[:, c:c + 1], None,
                                 ALU.add).then_inc(kt_ready, 1)
            project(0, 0)
            dve.wait_ge(kt_ready, C)
            for b in range(B):
                if b >= 1:
                    dve.wait_ge(kb_lo_done, b)
                for c in range(C):
                    last = v_.tensor_tensor(kb[:, c], kt[:, c, b].unsqueeze(1).to_broadcast([P, HC, KEYS]),
                                            ksel[:].unsqueeze(2).to_broadcast([P, HC, KEYS]), ALU.mult)
                last.then_inc(kb_raw_done, 1)
                dve.wait_ge(kb_hi_done, b + 1)
                if b >= 1:
                    dve.wait_ge(kb_stored, 32 * b)
                v_.tensor_tensor(kb_lo[:].rearrange("p c n -> p (c n)"), kb[:].rearrange("p c h k -> p (c h k)"),
                                 f32(kb_hi[:]).rearrange("p c n -> p (c n)"), ALU.subtract).then_inc(kb_lo_done, 1)
            for n in range(B * C):
                b, c = divmod(n, C)
                dve.wait_ge(vb_mm, n + 1)
                bank = (ps_pv, ps_q)[n % 2]
                v_.tensor_tensor(vb[:, b, c, :, :, 0:HD],
                                 bank[:, 0:NJ * NHMAX * HD].rearrange("p (j h d) -> p j h d", h=NHMAX, d=HD),
                                 vmask[:, :, :, 0:HD], ALU.mult).then_inc(vb_done, 1)
                v_.tensor_copy(vb[:, b, c, :, :, HD:], vmask[:, :, :, HD:]).then_inc(vb_done, 1)
            dve.wait_ge(mask_in, 32)
            masks(0, 0)
            masks(1, 1)
            maxima(0, range(3 * TG))
            maxima_parts(0, 0)
            stats_of(1)
            normalise(1)
            project(1, 1)

            def step(g, u, scores_next, project_next):
                if project_next:
                    stats_of(g + 2)
                if scores_next:
                    maxima(g + 1, range(0, 3))
                if project_next:
                    normalise(g + 2)
                if scores_next:
                    maxima(g + 1, range(3, 3 * TG))
                    maxima_parts(g + 1, 1 - u)
                heads(g, u)
                if project_next:
                    masks(g + 2, u)
                    project(g + 2, u)
                heads_transposed(g, 1)
                residual(g, 0)
                residual(g, 1)
                heads_transposed(g, 3)
                residual(g, 2)
                residual(g, 3)

            for g in range(2):
                step(g, g, True, True)
            with dve.Fori(2, NG - 3, 2) as r:
                for u in range(2):
                    step(r + u, u, True, True)
            step(NG - 2, 0, True, False)
            step(NG - 1, 1, False, False)

        @block.tensor
        def _(pe):
            mm_ = nc.tensor.matmul

            def transposed(bank, hi, lo):
                for n, part in enumerate((hi, lo)):
                    for c in range(C):
                        last = mm_(bank[:, n * C + c, :], part[:, c * P:(c + 1) * P], ident_r[:], start=True, stop=True)
                return last

            def split_product(dst, pairs):
                todo = [(l, r) for lh, ll, rh, rl in pairs for l, r in ((lh, rh), (ll, rh), (lh, rl))]
                for n, (l, r) in enumerate(todo):
                    last = mm_(dst, l, r, start=(n == 0), stop=(n == len(todo) - 1))
                return last

            pe.wait_ge(wattn_in, NATTN)
            for c in range(C):
                for k in range(C):
                    last = mm_(ps_sc[c][:, 0:B * KEYS], w_raw[:, K, k, c * P:(c + 1) * P], ctx_t[:, k],
                               start=(k == 0), stop=(k == C - 1))
                last.then_inc(prep_mm, 1)
            pe.wait_ge(zeroed, 5)
            for b in range(B):
                if b >= 2:
                    pe.wait_ge(v_ready, b - 1)
                dst = ps_mx[b % 2][0:KEYS, 0:D]
                for k in range(C):
                    mm_(dst, ctx_t[:, k, b * KEYS:(b + 1) * KEYS], w_raw[:, V, k], start=(k == 0), stop=False)
                mm_(dst, ones1[0:1, 0:KEYS], bv[0:1, :], start=False, stop=True).then_inc(prep_mm, 1)
            pe.wait_ge(consts_ready, 3)
            pe.wait_ge(w_lo_ready, 2)

            def project(g, u):
                pe.wait_ge(xn_lo_ready, g + 1)
                for i in range(TG):
                    if i == 1:
                        pe.wait_ge(mt_ready, g)
                    if i == 2:
                        pe.wait_ge(xnt_act, 2 * g + 1)
                    if i == 3:
                        pe.wait_ge(xnt_dve, 2 * g + 1)
                    transposed(ps_t[i % 2], xn_hi[:, i], xn_lo[:, i]).then_inc(xnt_filled, 1)
                pe.wait_ge(xnt_act, 2 * g + 2)
                pe.wait_ge(xnt_dve, 2 * g + 2)
                for c in range(C):
                    pe.wait_ge(q_lo_ready, C * g + c)
                    split_product(ps_q[:], [(w_hi[:, 0, k, c * P:(c + 1) * P], w_lo[:, 0, k, c * P:(c + 1) * P],
                                             xnt[:, :, k, :], xnt[:, :, C + k, :]) for k in range(C)]
                                  ).then_inc(q_filled, 1)

            def maxima(g, u, n):
                i, k = n // 3, n % 3
                h0, h1 = UNITS[k]
                bank = ps_mx[n % 2]
                mm_(bank[:, 0:(h1 - h0) * KEYS], ident_b[:],
                    mbias[:, u, i].unsqueeze(1).to_broadcast([P, h1 - h0, KEYS]), start=True, stop=True)
                for c in range(C):
                    lo, hi = max(h0, c * HC), min(h1, (c + 1) * HC)
                    if lo < hi:
                        last = mm_(bank[:, (lo - h0) * KEYS:(hi - h0) * KEYS], q_hi[:, u, c, i * P:(i + 1) * P],
                                   kmax[:, c, (lo - c * HC) * KEYS:(hi - c * HC) * KEYS],
                                   start=False, stop=True, skip_group_check=True)
                last.then_inc(mx_filled, 1)

            def maxima_begin(g):
                pe.wait_ge(q_hi_ready, C * (g + 1))
                pe.wait_ge(mask_ready, 2 * (g + 1))
                pe.wait_ge(kmax_in, (g // 2 + 1) * 16)

            def maxima_transposed(g):
                pe.wait_ge(mm_ready, g + 1)
                for i in range(TG):
                    last = mm_(ps_t[1][:, i, :], mm[:, i], ident_r[:], start=True, stop=True)
                last.then_inc(mt_filled, 1)

            def scores(g, u, n):
                c, j = divmod(n, NJ)
                rows = min(P, HK - j * P)
                dst = ps_sc[n % 2][0:rows]
                at = slice(j * P, j * P + rows)
                mm_(dst, sel_r[:, c, at], rhs_mm[:, u], start=True, stop=False)
                mm_(dst, kcur[:, 0, c, at], q_hi[:, u, c], start=False, stop=False)
                mm_(dst, kcur[:, 1, c, at], q_hi[:, u, c], start=False, stop=False)
                mm_(dst, kcur[:, 0, c, at], q_lo[:, u, c], start=False, stop=True).then_inc(sc_filled, 1)

            def values(g, t):
                pe.wait_ge(o_ready, TG * g + t)
                for n in range(C * NJ):
                    c, j = divmod(n, NJ)
                    rows = min(P, HK - j * P)
                    h0, nh = TILE_HEADS[j]
                    cols = slice((c * HC + h0) * VW, (c * HC + h0 + nh) * VW)
                    last = mm_(ps_pv[:, cols], pt[0:rows, n, t * P:(t + 1) * P],
                               vb[0:rows, bass.ds(g // 2, 1), c, j, 0:nh, :].rearrange("p o h v -> p (o h v)"),
                               start=(n == 0), stop=True, skip_group_check=True)
                last.then_inc(pv_filled, 1)

            def heads_transposed(g, t, projected):
                pe.wait_ge(o_lo_ready, TG * g + t + 1)
                if t >= 2:
                    pe.wait_ge((ot_act, ot_dve)[t % 2], 2 * g + 1)
                transposed(ps_t[t % 2], o_hi[:, t], o_lo[:, t]).then_inc(ot_filled, 1)

            def out_projection(g, t):
                pe.wait_ge((ot_act, ot_dve)[t % 2], 2 * g + t // 2 + 1)
                pe.wait_ge(x1_ready, TG * g + t)
                split_product(ps_q[:, 0:D], [(ot[:, t, k], ot[:, t, C + k], w_hi[:, 1, k], w_lo[:, 1, k])
                                             for k in range(C)]).then_inc(op_filled, 1)

            project(0, 0)
            pe.wait_ge(q_lo_ready, C)
            for n in range(B * C):
                b, c = divmod(n, C)
                pe.wait_ge(v_ready, b + 1)
                if n >= 2:
                    pe.wait_ge(vb_done, 2 * (n - 1))
                bank = (ps_pv, ps_q)[n % 2]
                for j, (h0, _) in enumerate(TILE_HEADS):
                    at = (c * HC + h0) * HD
                    last = mm_(bank[:, j * NHMAX * HD:(j + 1) * NHMAX * HD], sel_raw[0:KEYS, (c * NJ + j) * P:(c * NJ + j + 1) * P],
                               v_sb[:, b, at:at + NHMAX * HD], start=True, stop=True)
                last.then_inc(vb_mm, 1)
            maxima_begin(0)
            for n in range(3 * TG):
                if n >= 2:
                    pe.wait_ge(mx_used, n - 1)
                maxima(0, 0, n)
            maxima_transposed(0)
            pe.wait_ge(vb_done, 2 * B * C)
            project(1, 1)

            def step(g, u, scores_next, project_next):
                pe.wait_ge(mt_ready, g + 1)
                pe.wait_ge(q_lo_ready, C * (g + 1))
                pe.wait_ge(kcur_in, (g // 2 + 1) * 16)
                if scores_next:
                    maxima_begin(g + 1)
                unit = 0
                for n in range(C * NJ):
                    if isinstance(g, int) and g == 0 and n < 2:
                        pass
                    pe.wait_ge(exp_done, C * NJ * g + n - 1 if n >= 1 else C * NJ * g)
                    scores(g, u, n)
                    while scores_next and unit * C * NJ < 3 * TG * (n + 1):
                        pe.wait_ge(mx_used, 3 * TG * (g + 1) + unit - 1)
                        maxima(g + 1, 1 - u, unit)
                        unit += 1
                if scores_next:
                    maxima_transposed(g + 1)
                pe.wait_ge(exp_done, C * NJ * (g + 1))
                for t in range(TG):
                    values(g, t)
                if project_next:
                    project(g + 2, u)
                    pe.wait_ge(q_lo_ready, C * (g + 3))
                elif scores_next:
                    pe.wait_ge(mt_ready, g + 2)
                for t in (0, 2):
                    for n in (t, t + 1):
                        heads_transposed(g, n, project_next)
                    for n in (t, t + 1):
                        out_projection(g, n)

            for g in range(2):
                step(g, g, True, True)
            with pe.Fori(2, NG - 3, 2) as r:
                for u in range(2):
                    step(r + u, u, True, True)
            step(NG - 2, 0, True, False)
            step(NG - 1, 1, False, False)


def feed_forward(nc, a, out, x_res, ident):
    ctx = ExitStack()
    with ctx:
        def sb(name, shape, dt=F32):
            return ctx.enter_context(nc.sbuf_tensor(name, shape, dt))

        def ps(name, shape, dt=F32):
            return ctx.enter_context(nc.psum_tensor(name, shape, dt))

        def sem(name):
            return ctx.enter_context(nc.semaphore(name))

        def f32(ap):
            return ap.bitcast(F32)

        NU = (E + 2) // 2
        gu_hi = sb("gu_hi", [P, C, E + 2, 2 * DE], F32R)
        gu_lo = sb("gu_lo", [P, C, E + 2, 2 * DE], F32R)
        dn_hi = sb("dn_hi", [P, E + 2, D], F32R)
        dn_lo = sb("dn_lo", [P, E + 2, D], F32R)
        raw = sb("raw", [P, 2, C + 1, 2 * DE])
        r_raw = sb("r_raw", [P, C, E])
        r_hi = sb("r_hi", [P, C, E], F32R)
        r_lo = sb("r_lo", [P, C, E], F32R)
        x2_hi = sb("x2_hi", [P, NT, C, P], F32R)
        x2_lo = sb("x2_lo", [P, NT, C, P], F32R)
        stats = sb("stats2", [P, TG, 6])
        mv = sb("mv2", [P, TG, 2])
        ve = sb("ve2", [P, TG])
        rstd = sb("rstd2", [P, TG])
        pow_e = sb("pow_e2", [P, TG])
        hold = sb("hold2", [P, 1])
        xn = sb("xn2", [P, TG, D])
        rt = sb("rt", [P, GT])
        cur_hi = sb("cur_hi", [P, 2, C, P], F32R)
        cur_lo = sb("cur_lo", [P, 2, C, P], F32R)
        logit = sb("logit", [P, NT, E])
        iota = sb("iota", [P, NT, E])
        work = sb("work", [P, NT, E])
        prob = sb("prob", [P, NT, E])
        one1 = sb("one1", [P, NT, E])
        one2 = sb("one2", [P, NT, E])
        coef = sb("coef", [P, NT, E])
        top = sb("top", [P, NT])
        at1 = sb("at1", [P, NT])
        rsum = sb("rsum", [P, NT])
        sg = sb("sg", [P, 2, 2, DE])
        hid = sb("hid", [P, 2, 2, DE])
        ht_hi = sb("ht_hi", [P, 2, 2, P], F32R)
        ht_lo = sb("ht_lo", [P, 2, 2, P], F32R)

        ps_gu = [ps(f"ps_gu{i}", [P, 2, 2 * DE]) for i in range(2)]
        ps_ht = [ps(f"ps_ht{i}", [P, 2, P]) for i in range(2)]
        ps_y = [ps(f"ps_y{i}", [P, D]) for i in range(2)]
        ps_a = ps("ps_a", [P, 2, C, P])
        ps_b = ps("ps_b", [P, 512])

        w_in = [sem("w_in0"), sem("w_in1")]
        r_in = sem("r_in")
        w_hi_ready = sem("fw_hi_ready")
        w_lo_ready = sem("fw_lo_ready")
        r_parts = sem("r_parts")
        pow_ready = sem("pow_ready")
        stat_step = sem("f_stat_step")
        aggr_step = sem("f_aggr_step")
        stats_ready = sem("f_stats_ready")
        rstd_ready = sem("f_rstd_ready")
        xn_ready = sem("f_xn_ready")
        xt_filled = sem("xt_filled")
        x2_hi_ready = sem("x2_hi_ready")
        x2_lo_ready = sem("x2_lo_ready")
        rt_filled = sem("rt_filled")
        rt_ready = sem("rt_ready")
        lg_filled = sem("lg_filled")
        lg_ready = sem("lg_ready")
        iota_ready = sem("iota_ready")
        route_step = sem("route_step")
        shifted = sem("shifted")
        exped = sem("exped")
        gu_filled = sem("gu_filled")
        cur_ready = sem("cur_ready")
        silu_ready = sem("silu_ready")
        h_ready = sem("h_ready")
        ht_filled = sem("ht_filled")
        ht_hi_ready = sem("ht_hi_ready")
        ht_lo_ready = sem("ht_lo_ready")
        dn_filled = sem("dn_filled")
        y_used = sem("y_used")
        out_done = sem("out_done")

        out_v = out.rearrange("b (g p i) d -> (b g) p i d", p=P, i=TG)
        block = ctx.enter_context(nc.Block())

        @block.sync
        def _(sp):
            sp.dma_start(r_raw[:], a["router"].rearrange("(c p) e -> p c e", p=P)).then_inc(r_in, 16)
            order = [E, E + 1] + list(range(E))
            for n, e in enumerate(order):
                s = n % 2
                if n >= 2:
                    sp.wait_ge(w_lo_ready, 2 * (n - 1))
                if e < E:
                    gate, up, down = a["eg"][e], a["eu"][e], a["ed"][e]
                else:
                    at = slice((e - E) * DE, (e - E + 1) * DE)
                    gate, up, down = a["sgate"][:, at], a["sup"][:, at], a["sdown"][at, :]
                sp.dma_start(raw[:, s, 0:C, 0:DE], gate.rearrange("(c p) d -> p c d", p=P)).then_inc(w_in[s], 16)
                sp.dma_start(raw[:, s, 0:C, DE:], up.rearrange("(c p) d -> p c d", p=P)).then_inc(w_in[s], 16)
                sp.dma_start(raw[:, s, C, :], down).then_inc(w_in[s], 16)
            for g in range(NG):
                sp.wait_ge(y_used, TG * (g + 1))
                sp.dma_start(out_v[g], x_res[:, g * TG:(g + 1) * TG, :]).then_inc(out_done, 16)
            sp.wait_ge(out_done, 16 * NG)

        order = [E, E + 1] + list(range(E))

        @block.gpsimd
        def _(pool):
            g_ = nc.gpsimd
            g_.memset(pow_e[:], -0.5).then_inc(pow_ready, 1)
            g_.iota(iota[:], [[0, NT], [1, E]], base=-E, channel_multiplier=0,
                    allow_small_or_imprecise_dtypes=True).then_inc(iota_ready, 1)
            g_.memset(rt[:], 0.0).then_inc(pow_ready, 1)
            pool.wait_ge(pow_ready, 2)
            def rows(g):
                pool.wait_ge(stats_ready, g + 1)
                g_.tensor_tensor(rstd[:], ve[:], pow_e[:], ALU.pow).then_inc(rstd_ready, 1)

            rows(0)
            with pool.Fori(1, NG) as g:
                rows(g)

            def current(t, u):
                for dst, src in ((cur_hi, x2_hi), (cur_lo, x2_lo)):
                    g_.tensor_copy(dst[:, u], f32(src[:, bass.ds(t, 1)]).rearrange("p o c q -> p (o c) q")
                                   ).then_inc(cur_ready, 1)

            pool.wait_ge(x2_lo_ready, 2 * NG)
            current(0, 0)
            current(1, 1)
            with pool.Fori(0, NT - 3, 2) as r:
                for u in range(2):
                    pool.wait_ge(gu_filled, NU * (r + u + 1))
                    current(r + u + 2, u)

        @block.scalar
        def _(act):
            def copy(dst, src):
                return nc.scalar.activation(dst, src, ACT.Copy)

            act.wait_ge(r_in, 16)
            copy(r_hi[:], r_raw[:]).then_inc(r_parts, 1)

            def rows(g):
                for i in range(0, TG, 2):
                    act.wait_ge(xt_filled, 2 * g + i // 2 + 1)
                    copy(x2_hi[:, bass.ds(g * TG + i, 2)], ps_a[:]).then_inc(x2_hi_ready, 1)
                act.wait_ge(rt_filled, g + 1)
                copy(rt[0:E], ps_b[0:E, :]).then_inc(rt_ready, 1)

            rows(0)
            with act.Fori(1, NG) as g:
                rows(g)

            act.wait_ge(shifted, 1)
            nc.scalar.activation(prob[:], work[:], ACT.Exp).then_inc(exped, 1)
            for n, e in enumerate(order):
                act.wait_ge(w_in[n % 2], 48 * (n // 2 + 1))
                copy(gu_hi[:, :, e], raw[:, n % 2, 0:C]).then_inc(w_hi_ready, 1)
                copy(dn_hi[:, e], raw[:, n % 2, C]).then_inc(w_hi_ready, 1)

            def silu(n, b):
                act.wait_ge(gu_filled, n + 1)
                nc.scalar.activation(sg[:, b], ps_gu[b][:, :, 0:DE], ACT.Silu).then_inc(silu_ready, 1)

            def hidden(n, b):
                act.wait_ge(ht_filled, n + 1)
                copy(ht_hi[:, b], ps_ht[b][:]).then_inc(ht_hi_ready, 1)

            def step(t, u, first):
                for m in range(NU):
                    n, b = NU * t + m, (NU * u + m) % 2
                    silu(n, b)
                    if not (first and m == 0):
                        hidden(n - 1, 1 - b)

            step(0, 0, True)
            step(1, 1, False)
            step(2, 0, False)
            with act.Fori(3, NT - 1, 2) as r:
                step(r, 1, False)
                step(r + 1, 0, False)
            step(NT - 1, 1, False)
            hidden(NU * NT - 1, (NU * NT - 1) % 2)

        @block.vector
        def _(dve):
            v_ = nc.vector
            dve.wait_ge(r_parts, 1)
            v_.tensor_tensor(r_lo[:], r_raw[:], f32(r_hi[:]), ALU.subtract).then_inc(r_parts, 1)

            def rows(g):
                def row(i):
                    return x_res[:, bass.ds(g * TG + i, 1), :].rearrange("p o d -> p (o d)")
                for i in range(TG):
                    v_.bn_stats(stats[:, i], row(i)).then_inc(stat_step, 1)
                dve.wait_ge(stat_step, TG * (g + 1))
                v_.memset(hold[:], 0.0)
                for i in range(TG):
                    v_.bn_aggr(mv[:, i], stats[:, i]).then_inc(aggr_step, 1)
                dve.wait_ge(aggr_step, TG * (g + 1))
                v_.tensor_scalar(ve[:], mv[:, :, 1], EPS, None, ALU.add).then_inc(stats_ready, 1)
                dve.wait_ge(rstd_ready, g + 1)
                dve.wait_ge(xt_filled, 2 * g)
                for i in range(TG):
                    last = v_.tensor_scalar(xn[:, i], row(i), mv[:, i, 0:1], rstd[:, i:i + 1], ALU.subtract, ALU.mult)
                last.then_inc(xn_ready, 1)
                for i in range(0, TG, 2):
                    dve.wait_ge(x2_hi_ready, 2 * g + i // 2 + 1)
                    v_.tensor_tensor(x2_lo[:, bass.ds(g * TG + i, 2)].rearrange("p t c q -> p (t c q)"),
                                     ps_a[:].rearrange("p t c q -> p (t c q)"),
                                     f32(x2_hi[:, bass.ds(g * TG + i, 2)]).rearrange("p t c q -> p (t c q)"),
                                     ALU.subtract).then_inc(x2_lo_ready, 1)
                dve.wait_ge(lg_filled, g + 1)
                v_.tensor_copy(logit[:, bass.ds(g * TG, TG)], ps_b[:].rearrange("p (t e) -> p t e", e=P)[:, :, 0:E]
                               ).then_inc(lg_ready, 1)

            rows(0)
            with dve.Fori(1, NG) as g:
                rows(g)

            steps = [0]

            def link(ins):
                steps[0] += 1
                ins.then_inc(route_step, 1)
                dve.wait_ge(route_step, steps[0])

            def spread(ap):
                return ap.unsqueeze(2).to_broadcast([P, NT, E])

            def choose(values, one):
                link(v_.tensor_reduce(top[:], values[:], AX.X, ALU.max))
                link(v_.tensor_tensor(one[:], values[:], spread(top[:]), ALU.is_equal))
                link(v_.scalar_tensor_tensor(one[:], one[:], -float(E), iota[:], ALU.mult, ALU.add))
                link(v_.tensor_reduce(at1[:], one[:], AX.X, ALU.min))
                link(v_.tensor_scalar(at1[:], at1[:], -float(E) - 1.0, float(E), ALU.min, ALU.add))
                link(v_.tensor_tensor(one[:], iota[:], spread(at1[:]), ALU.is_equal))

            dve.wait_ge(lg_ready, NG)
            dve.wait_ge(iota_ready, 1)
            choose(logit, one1)
            v_.tensor_tensor(work[:], logit[:], spread(top[:]), ALU.subtract).then_inc(shifted, 1)
            link(v_.scalar_tensor_tensor(one2[:], one1[:], -3e38, logit[:], ALU.mult, ALU.add))
            link(v_.tensor_copy(coef[:], one2[:]))
            choose(coef, one2)
            dve.wait_ge(exped, 1)
            link(v_.tensor_reduce(rsum[:], prob[:], AX.X, ALU.add))
            link(v_.reciprocal(rsum[:], rsum[:]))
            link(v_.tensor_tensor(prob[:], prob[:], spread(rsum[:]), ALU.mult))
            link(v_.tensor_tensor(coef[:], one1[:], one2[:], ALU.add))
            link(v_.tensor_tensor(coef[:], coef[:], prob[:], ALU.mult))

            for n, e in enumerate(order):
                dve.wait_ge(w_hi_ready, 2 * n + 2)
                v_.tensor_tensor(gu_lo[:, :, e], raw[:, n % 2, 0:C], f32(gu_hi[:, :, e]), ALU.subtract).then_inc(w_lo_ready, 1)
                v_.tensor_tensor(dn_lo[:, e], raw[:, n % 2, C], f32(dn_hi[:, e]), ALU.subtract).then_inc(w_lo_ready, 1)

            def gated(n, b, t, m):
                dve.wait_ge(silu_ready, n + 1)
                if not isinstance(n, int) or n >= 2:
                    dve.wait_ge(ht_filled, n - 1)
                if m == NU - 1:
                    v_.tensor_tensor(hid[:, b], sg[:, b], ps_gu[b][:, :, DE:], ALU.mult).then_inc(h_ready, 2)
                else:
                    for k in range(2):
                        v_.scalar_tensor_tensor(hid[:, b, k], sg[:, b, k],
                                                coef[:, bass.ds(t, 1), 2 * m + k:2 * m + k + 1].rearrange("p o e -> p (o e)"),
                                                ps_gu[b][:, k, DE:], ALU.mult, ALU.mult).then_inc(h_ready, 1)

            def hidden(n, b):
                dve.wait_ge(ht_hi_ready, n + 1)
                v_.tensor_tensor(ht_lo[:, b], ps_ht[b][:], f32(ht_hi[:, b]), ALU.subtract).then_inc(ht_lo_ready, 1)

            def finish(t, u):
                dve.wait_ge(dn_filled, NU * (t + 1))
                at = x_res[:, bass.ds(t, 1), :].rearrange("p o d -> p (o d)")
                v_.tensor_tensor(at, ps_y[u][:], at, ALU.add).then_inc(y_used, 1)

            def step(t, u, first):
                for m in range(NU):
                    n, b = NU * t + m, (NU * u + m) % 2
                    gated(n, b, t, m)
                    if not (first and m == 0):
                        hidden(n - 1, 1 - b)
                    if m == 2 and not first:
                        finish(t - 1, 1 - u)

            step(0, 0, True)
            step(1, 1, False)
            step(2, 0, False)
            with dve.Fori(3, NT - 1, 2) as r:
                step(r, 1, False)
                step(r + 1, 0, False)
            step(NT - 1, 1, False)
            hidden(NU * NT - 1, (NU * NT - 1) % 2)
            finish(NT - 1, 1)

        @block.tensor
        def _(pe):
            mm_ = nc.tensor.matmul
            pe.wait_ge(r_parts, 2)
            def rows(g):
                pe.wait_ge(xn_ready, g + 1)
                for i in range(0, TG, 2):
                    pe.wait_ge(x2_lo_ready, 2 * g + i // 2)
                    for k in range(2):
                        for c in range(C):
                            last = nc.tensor.transpose(ps_a[:, k, c], xn[:, i + k, c * P:(c + 1) * P], ident[:])
                    last.then_inc(xt_filled, 1)
                pe.wait_ge(x2_lo_ready, 2 * g + 2)
                pe.wait_ge(lg_ready, g)
                n = 0
                for k in range(C):
                    for w, x in ((r_hi, x2_hi), (r_lo, x2_hi), (r_hi, x2_lo)):
                        last = mm_(ps_b[0:E, :], w[:, k], x[:, bass.ds(g * TG, TG), k], start=(n == 0), stop=(n == 5))
                        n += 1
                last.then_inc(rt_filled, 1)
                pe.wait_ge(rt_ready, g + 1)
                for i in range(TG):
                    last = nc.tensor.transpose(ps_b[:, i * P:(i + 1) * P], rt[:, i * P:(i + 1) * P], ident[:])
                last.then_inc(lg_filled, 1)

            rows(0)
            with pe.Fori(1, NG) as g:
                rows(g)

            pe.wait_ge(w_lo_ready, 2 * (E + 2))

            def gate_up(t, u, n, b, m):
                if not isinstance(n, int) or n >= 2:
                    pe.wait_ge(h_ready, 2 * (n - 1))
                dst = ps_gu[b][:].rearrange("p e d -> p (e d)")
                i = 0
                for k in range(C):
                    for x, w in ((cur_hi, gu_hi), (cur_lo, gu_hi), (cur_hi, gu_lo)):
                        last = mm_(dst, x[:, u, k],
                                   w[:, k, 2 * m:2 * m + 2].rearrange("p e d -> p (e d)"), start=(i == 0), stop=(i == 5))
                        i += 1
                last.then_inc(gu_filled, 1)

            def hidden(n, b):
                pe.wait_ge(h_ready, 2 * (n + 1))
                if not isinstance(n, int) or n >= 2:
                    pe.wait_ge(ht_lo_ready, n - 1)
                for k in range(2):
                    last = nc.tensor.transpose(ps_ht[b][:, k], hid[:, b, k], ident[:])
                last.then_inc(ht_filled, 1)

            def down(t, u, n, b, m):
                pe.wait_ge(ht_lo_ready, n + 1)
                if m == 0 and (not isinstance(t, int) or t >= 2):
                    pe.wait_ge(y_used, t - 1)
                i = 0
                for k in range(2):
                    for x, w in ((ht_hi, dn_hi), (ht_lo, dn_hi), (ht_hi, dn_lo)):
                        last = mm_(ps_y[u][:], x[:, b, k], w[:, 2 * m + k], start=(m == 0 and i == 0),
                                   stop=(m == NU - 1 and i == 5))
                        i += 1
                last.then_inc(dn_filled, 1)

            def step(t, u, first):
                for m in range(NU):
                    n, b = NU * t + m, (NU * u + m) % 2
                    if m == 0:
                        pe.wait_ge(cur_ready, 2 * (t + 1))
                    gate_up(t, u, n, b, m)
                    if not (first and m < 2):
                        if m >= 2:
                            down(t, u, n - 2, b, m - 2)
                        else:
                            down(t - 1, 1 - u, n - 2, b, m + NU - 2)
                    if not (first and m == 0):
                        hidden(n - 1, 1 - b)

            step(0, 0, True)
            step(1, 1, False)
            step(2, 0, False)
            with pe.Fori(3, NT - 1, 2) as r:
                step(r, 1, False)
                step(r + 1, 0, False)
            step(NT - 1, 1, False)
            n = NU * NT
            down(NT - 1, 1, n - 2, n % 2, NU - 2)
            hidden(n - 1, (n - 1) % 2)
            down(NT - 1, 1, n - 1, (n - 1) % 2, NU - 1)


_NAMES = {"x": "x", "wq": "L0_xattn_wq", "wk": "L0_xattn_wk", "wv": "L0_xattn_wv", "wo": "L0_xattn_wo",
          "router": "L0_ffn_router", "eg": "L0_ffn_experts_gate", "eu": "L0_ffn_experts_up",
          "ed": "L0_ffn_experts_down", "sgate": "L0_ffn_shared_gate", "sup": "L0_ffn_shared_up",
          "sdown": "L0_ffn_shared_down"}


def kernel(**inputs):
    import concourse.bacc as _bacc
    from concourse.bass_utils import run_bass_kernel_spmd as _run

    f = {k: np.ascontiguousarray(np.asarray(v)) for k, v in inputs.items()}
    arrays = {n: f[k] for n, k in _NAMES.items()}
    arrays["ctx_t"] = np.ascontiguousarray(f["ctx_1024"].transpose(2, 0, 1).reshape(D, B * KEYS))
    for n in ("bq", "bk"):
        arrays[n] = np.ascontiguousarray(f["L0_xattn_" + n].reshape(C, P).T)
    for n in ("bv", "bo"):
        arrays[n] = f["L0_xattn_" + n].reshape(1, D)
    m = f["mask_Bx1xSxS2_bk1"].reshape(NG, P, TG, KEYS)
    arrays["mask_tok"] = m.reshape(NG, P, TG * KEYS)
    arrays["mask_key"] = np.ascontiguousarray(m.transpose(0, 3, 2, 1).reshape(NG, KEYS, GT))
    arrays.update(constants())
    nc = _bacc.Bacc("TRN2", target_bir_lowering=False, num_devices=1)
    aps = {n: nc.dram_tensor(n + "_d", v.shape, mybir.dt.from_np(v.dtype), kind="ExternalInput").ap()
           for n, v in arrays.items()}
    out = nc.dram_tensor("out_d", (B, S, D), F32, kind="ExternalOutput").ap()
    kscr = nc.dram_tensor("k_blocks", (B, 2, P, C, HK), F32, kind="Internal").ap()
    build(nc, aps, out, kscr)
    r = _run(nc, [{n + "_d": v for n, v in arrays.items()}], core_ids=[0])
    return r.results[0]["out_d"]
```

```python
from contextlib import ExitStack

import numpy as np
import concourse.bass as bass
from concourse import mybir

F32 = mybir.dt.float32
F32R = mybir.dt.float32r
BF16 = mybir.dt.bfloat16
F16 = mybir.dt.float16
U8 = mybir.dt.uint8
ALU = mybir.AluOpType
ACT = mybir.ActivationFunctionType
AX = mybir.AxisListType

B, S, D = 4, 1024, 256
KEYS, HEADS, HD = 77, 16, 16
E, DE, DS = 8, 128, 256
P = 128
C = D // P
HC = HEADS // C
GT = 512
TG = GT // P
NG = B * S // GT
NT = B * S // P
HK = HC * KEYS
NJ = (HK + P - 1) // P
VW = HD + 1
MASKED = -(2.0 ** 120)
EPS = 1e-5
MROW = 96
HC_UNIT = 6
UNITS = [(0, 6), (6, 12), (12, 16)]
TILE_HEADS = [(P * j // KEYS, min(P * (j + 1) - 1, HK - 1) // KEYS - P * j // KEYS + 1) for j in range(NJ)]
NHMAX = max(n for _, n in TILE_HEADS)


def constants():
    f = np.arange(NJ * P)
    head, key = f // KEYS, f % KEYS
    live = f < HK
    sel = np.zeros((P, C, NJ * P), np.float32)
    for c in range(C):
        sel[key[live], c, f[live]] = 1.0
        sel[MROW + head[live] + c * HC, c, f[live]] = -1.0
        sel[MROW + HEADS + head[live] + c * HC, c, f[live]] = -1.0
    vmask = np.zeros((P, NJ, NHMAX), np.float32)
    for j, (h0, n) in enumerate(TILE_HEADS):
        for h in range(n):
            rows = f[(f // P == j) & live & (head == h0 + h)]
            vmask[rows % P, j, h] = 1.0
    ksel = np.zeros((P, HC), np.float32)
    ksel[np.arange(P), np.arange(P) // HD] = 1.0 / np.sqrt(HD)
    return {"c_sel": sel.reshape(P, -1), "c_vmask": vmask.reshape(P, -1), "c_ksel": ksel,
            "c_ident": np.eye(P, dtype=np.float32)}


def build(nc, a, out, kscr):
    with nc.sbuf_tensor("x_res", [P, NT, D], F32) as x_res, nc.sbuf_tensor("ident", [P, P], F32) as ident:
        attention(nc, a, kscr, x_res, ident)
        feed_forward(nc, a, out, x_res, ident)


def attention(nc, a, kscr, x_res, ident):
    ctx = ExitStack()
    with ctx:
        def sb(name, shape, dt=F32):
            return ctx.enter_context(nc.sbuf_tensor(name, shape, dt))

        def ps(name, shape, dt=F32):
            return ctx.enter_context(nc.psum_tensor(name, shape, dt))

        def sem(name):
            return ctx.enter_context(nc.semaphore(name))

        def f32(ap):
            return ap.bitcast(F32)

        ident_b = sb("ident_b", [P, P], BF16)
        sel_raw = sb("sel_raw", [P, C * NJ * P])
        sel_r = sb("sel_r", [P, C, NJ * P], F32R)
        sel_b = sb("sel_b", [KEYS, C, NJ * P], BF16)
        vmask = sb("vmask", [P, NJ, NHMAX])
        ksel = sb("ksel", [P, HC])
        w_raw = sb("w_raw", [P, 4, C, D])
        w_hi = sb("w_hi", [P, 2, C, D], F32R)
        w_lo = sb("w_lo", [P, 2, C, D], F32R)
        bq = sb("bq", [P, C])
        bk = sb("bk", [P, C])
        bv = sb("bv", [1, D])
        bo = sb("bo", [P, D])
        ones1 = sb("ones1", [1, P])
        ctx_t = sb("ctx_t", [P, C, B * KEYS])
        kt = sb("kt", [P, C, B, KEYS])
        v_part = sb("v_part", [KEYS, B, HEADS + 1, 3, VW], BF16)
        v_rest = sb("v_rest", [KEYS, B, D])
        vb = sb("vb", [P, B, C, NJ, NHMAX, 3, VW], BF16)
        kb = sb("kb", [P, C, HC, KEYS])
        kb_part = sb("kb_part", [P, 2, C, HK], F32R)
        kcur = sb("kcur", [P, 2, C, HK], F32R)
        kmax = sb("kmax", [P, C, HK], F32R)
        mk_raw = sb("mk_raw", [P, NG, TG * KEYS], U8)
        mt_raw = sb("mt_raw", [KEYS, NG, GT], U8)
        hold = sb("hold", [P, 1])
        mbias = sb("mbias", [P, 2, TG, KEYS], BF16)
        rhs_mm = sb("rhs_mm", [P, 2, GT], F32R)
        stats = sb("stats", [P, TG, 6])
        mv = sb("mv", [P, TG, 2])
        ve = sb("ve", [P, TG])
        rstd = sb("rstd", [P, TG])
        pow_e = sb("pow_e", [P, TG])
        negm = sb("anegm", [P, TG])
        xc = sb("axc", [P, TG, D])
        xn = sb("xn", [P, TG, D])
        xnt_hi = sb("xnt_hi", [P, TG, C, P], F32R)
        xnt_lo = sb("xnt_lo", [P, TG, C, P], F32R)
        q_hi = sb("q_hi", [P, 2, C, GT], F32R)
        q_lo = sb("q_lo", [P, 2, C, GT], F32R)
        mx = sb("mx", [P, TG, HEADS])
        mm = sb("mm", [P, TG, 2 * HEADS], F32R)
        pf = sb("pf", [P, 2, GT])
        p_hi = sb("p_hi", [P, C * NJ, GT], F16)
        p_lo = sb("p_lo", [P, C * NJ, GT], BF16)
        allmasked = sb("allmasked", [P, TG, HEADS])
        nanfix = sb("nanfix", [P, 2, TG, HEADS])
        den = sb("den", [P, TG, HEADS])
        rden = sb("rden", [P, TG, HEADS])
        o = sb("o", [P, TG, D])
        ot_hi = sb("ot_hi", [P, TG, C, P], F32R)
        ot_lo = sb("ot_lo", [P, TG, C, P], F32R)

        ps_mx = [ps(f"ps_mx{i}", [P, 512]) for i in range(2)]
        ps_sc = [ps(f"ps_sc{i}", [P, GT]) for i in range(2)]
        ps_t = [ps(f"ps_t{i}", [P, 2, C, P]) for i in range(2)]
        ps_q = [ps(f"ps_q{i}", [P, 512]) for i in range(2)]

        const_in = sem("const_in")
        wattn_in = sem("wattn_in")
        x_in = sem("x_in")
        mask_in = sem("mask_in")
        consts_ready = sem("consts_ready")
        w_hi_ready = sem("w_hi_ready")
        w_lo_ready = sem("w_lo_ready")
        zeroed = sem("zeroed")
        rhs_zeroed = sem("rhs_zeroed")
        kt_mm = sem("kt_mm")
        kt_ready = sem("kt_ready")
        v_mm = sem("v_mm")
        v1_ready = sem("v1_ready")
        r1_ready = sem("r1_ready")
        v2_ready = sem("v2_ready")
        v3_ready = sem("v3_ready")
        kb_raw_done = sem("kb_raw_done")
        kb_hi_done = sem("kb_hi_done")
        kb_lo_done = sem("kb_lo_done")
        kb_stored = sem("kb_stored")
        vb_mm = sem("vb_mm")
        vb_done = sem("vb_done")
        kmax_in = sem("kmax_in")
        kcur_in = sem("kcur_in")
        mask_ready = sem("mask_ready")
        stats_ready = sem("stats_ready")
        rstd_ready = sem("rstd_ready")
        stat_step = sem("stat_step")
        aggr_step = sem("aggr_step")
        xc_ready = sem("axc_ready")
        xn_ready = sem("xn_ready")
        xb_ready = sem("xb_ready")
        xt_filled = sem("xt_filled")
        xt_hi_ready = sem("xt_hi_ready")
        xt_lo_ready = sem("xt_lo_ready")
        q_filled = sem("q_filled")
        q_hi_ready = sem("q_hi_ready")
        q_lo_ready = sem("q_lo_ready")
        mx_filled = sem("mx_filled")
        mx_used = sem("mx_used")
        mx_hi_step = sem("mx_hi_step")
        mm_ready = sem("mm_ready")
        mt_filled = sem("mt_filled")
        mt_ready = sem("mt_ready")
        nan_step = sem("nan_step")
        nan_ready = sem("nan_ready")
        sc_filled = sem("sc_filled")
        p_hi_ready = sem("p_hi_ready")
        pf_ready = sem("pf_ready")
        p_lo_ready = sem("p_lo_ready")
        pv_filled = sem("pv_filled")
        den_step = sem("den_step")
        rden_step = sem("rden_step")
        o_ready = sem("o_ready")
        ot_filled = sem("ot_filled")
        ot_hi_ready = sem("ot_hi_ready")
        ot_lo_ready = sem("ot_lo_ready")
        op_filled = sem("op_filled")
        x1_ready = sem("x1_ready")

        x_v = a["x"].rearrange("b (g p i) d -> (b g) p i d", p=P, i=TG)
        mk_v = a["mask_tok"]
        mt_v = a["mask_key"]
        Q, K, V, O = range(4)

        NCONST = 16 * 4
        NATTN = 16 * (4 + 4 + 1)

        QUOTA = [-(-3 * TG * j // (C * NJ - 1)) for j in range(C * NJ)]

        block = ctx.enter_context(nc.Block())

        @block.sync
        def _(sp):
            def load_x(g):
                if g:
                    sp.wait_ge(x_in, 16 * g)
                sp.dma_start(x_res[:, g * TG:(g + 1) * TG, :], x_v[g]).then_inc(x_in, 16)

            load_x(0)
            sp.dma_start(mk_raw[:], mk_v.rearrange("g p k -> p g k")).then_inc(mask_in, 16)
            sp.dma_start(mt_raw[:], mt_v.rearrange("g k t -> k g t")).then_inc(mask_in, 16)
            sp.dma_start(ident[:], a["c_ident"]).then_inc(const_in, 16)
            for i, name in enumerate(("wq", "wk", "wv", "wo")):
                sp.dma_start(w_raw[:, i], a[name].rearrange("(c p) n -> p c n", p=P)).then_inc(wattn_in, 16)
            sp.dma_start(ctx_t[:], a["ctx_t"].rearrange("(c p) n -> p c n", p=P)).then_inc(wattn_in, 16)
            sp.dma_start(bq[:], a["bq"]).then_inc(wattn_in, 16)
            sp.dma_start(bk[:], a["bk"]).then_inc(wattn_in, 16)
            sp.dma_start(bv[:], a["bv"]).then_inc(wattn_in, 16)
            sp.dma_start(bo[:], a["bo"].to_broadcast([P, D])).then_inc(wattn_in, 16)
            sp.dma_start(sel_raw[:], a["c_sel"]).then_inc(const_in, 16)
            sp.dma_start(vmask[:].rearrange("p j h -> p (j h)"), a["c_vmask"]).then_inc(const_in, 16)
            sp.dma_start(ksel[:], a["c_ksel"]).then_inc(const_in, 16)
            for g in range(1, NG):
                load_x(g)
            for b in range(1, B):
                sp.wait_ge(kb_lo_done, b + 1)
                sp.dma_start(kscr[b], f32(kb_part[:]).rearrange("p h c n -> p (h c n)")).then_inc(kb_stored, 16)
                if b == 1:
                    sp.wait_ge(kb_stored, 16)
                    sp.wait_ge(mx_filled, 3 * TG * 2)
                    sp.dma_start(f32(kmax[:]).rearrange("p c n -> p (c n)"), kscr[1, :, 0:C * HK]).then_inc(kmax_in, 16)
            sp.wait_ge(kb_stored, 16 * (B - 1))
            for b in range(1, B):
                if b > 1:
                    sp.wait_ge(mx_filled, 3 * TG * 2 * b)
                    sp.dma_start(f32(kmax[:]).rearrange("p c n -> p (c n)"), kscr[b, :, 0:C * HK]).then_inc(kmax_in, 16)
                sp.wait_ge(sc_filled, C * NJ * 2 * b)
                sp.dma_start(f32(kcur[:]).rearrange("p h c n -> p (h c n)"), kscr[b]).then_inc(kcur_in, 16)

        @block.gpsimd
        def _(pool):
            g_ = nc.gpsimd
            g_.memset(ones1[:], 1.0).then_inc(zeroed, 1)
            g_.memset(pow_e[:], -0.5).then_inc(zeroed, 1)
            g_.memset(v_part[:], 0.0).then_inc(zeroed, 1)
            pool.wait_ge(zeroed, 3)
            g_.memset(v_part[:, :, 0:HEADS, 0, HD:], 1.0).then_inc(zeroed, 1)

            def norm(g):
                pool.wait_ge(stats_ready, g + 1)
                g_.tensor_tensor(rstd[:], ve[:], pow_e[:], ALU.pow).then_inc(rstd_ready, 1)

            def biased(g):
                pool.wait_ge(xn_ready, 2 * g + 2)
                for i in range(TG):
                    at = x_res[:, bass.ds(g * TG + i, 1), :].rearrange("p o d -> p (o d)")
                    g_.tensor_tensor(at, at, bo[:], ALU.add).then_inc(xb_ready, 1)

            norm(0)
            pool.wait_ge(wattn_in, NATTN)
            biased(0)
            norm(1)
            biased(1)
            norm(2)
            biased(2)
            with pool.Fori(3, NG) as g:
                norm(g)
                biased(g)

        @block.scalar
        def _(act):
            def copy(dst, src):
                return nc.scalar.activation(dst, src, ACT.Copy)

            def normalise(g, k):
                act.wait_ge(rstd_ready, g + 1)
                if not (isinstance(g, int) and g == 0):
                    act.wait_ge(xt_filled, 2 * g)
                for i in (2 * k, 2 * k + 1):
                    at = x_res[:, bass.ds(g * TG + i, 1), :].rearrange("p o d -> p (o d)")
                    last = nc.scalar.activation(xc[:, i], at, ACT.Identity, bias=negm[:, i:i + 1])
                last.then_inc(xc_ready, 1)
                act.wait_ge(xc_ready, 2 * g + k + 1)
                for i in (2 * k, 2 * k + 1):
                    last = nc.scalar.activation(xn[:, i], xc[:, i], ACT.Copy, scale=rstd[:, i:i + 1])
                last.then_inc(xn_ready, 1)

            def rows_high(g):
                act.wait_ge(q_filled, C * g)
                for k in range(2):
                    act.wait_ge(xt_filled, 2 * g + k + 1)
                    copy(xnt_hi[:, 2 * k:2 * k + 2], ps_t[k][:]).then_inc(xt_hi_ready, 1)

            def queries_high(g, u):
                for c in range(C):
                    act.wait_ge(q_filled, C * g + c + 1)
                    nc.scalar.activation(q_hi[:, u, c], ps_q[c][:], ACT.Identity, bias=bq[:, c:c + 1]).then_inc(q_hi_ready, 1)

            act.wait_ge(rstd_ready, 1)
            normalise(0, 0)
            normalise(0, 1)
            act.wait_ge(wattn_in, NATTN)
            copy(w_hi[:, 0], w_raw[:, Q]).then_inc(w_hi_ready, 1)
            copy(w_hi[:, 1], w_raw[:, O]).then_inc(w_hi_ready, 1)

            def keys_high(b):
                act.wait_ge(kb_raw_done, b + 1)
                if b >= 2:
                    act.wait_ge(kb_stored, 16 * (b - 1))
                dst = kb_part if b else kcur
                src = kb[:].rearrange("p c h k -> p c (h k)")
                copy(dst[:, 0], src).then_inc(kb_hi_done, 1)
                if b == 0:
                    copy(kmax[:], src).then_inc(kb_hi_done, 1)

            def exps(g, j):
                rows = min(P, HK - (j % NJ) * P)
                act.wait_ge(sc_filled, C * NJ * g + j + 1)
                if not (isinstance(g, int) and g == 0):
                    act.wait_ge(pv_filled, TG * g)
                nc.scalar.activation(p_hi[0:rows, j], ps_sc[j % 2][0:rows], ACT.Exp).then_inc(p_hi_ready, 1)
                if not (isinstance(g, int) and g == 0 and j < 2):
                    act.wait_ge(p_lo_ready, C * NJ * g + j - 1)
                nc.scalar.activation(pf[0:rows, j % 2], ps_sc[j % 2][0:rows], ACT.Exp).then_inc(pf_ready, 1)

            def heads_transposed(g):
                for k in range(2):
                    act.wait_ge(ot_filled, 2 * g + k + 1)
                    copy(ot_hi[:, 2 * k:2 * k + 2], ps_t[k][:]).then_inc(ot_hi_ready, 1)

            act.wait_ge(const_in, NCONST)
            copy(ident_b[:], ident[:]).then_inc(consts_ready, 1)
            keys_high(0)
            rows_high(0)
            queries_high(0, 0)
            copy(sel_b[:].rearrange("p c n -> p (c n)"), sel_raw[0:KEYS]).then_inc(consts_ready, 1)
            copy(sel_r[:].rearrange("p c n -> p (c n)"), sel_raw[:]).then_inc(consts_ready, 1)
            act.wait_ge(zeroed, 4)
            for n in range(2):
                act.wait_ge(v_mm, n + 1)
                for k in range(2):
                    last = copy(v_part[:, 2 * n + k, 0:HEADS, 0, 0:HD],
                                ps_mx[n][0:KEYS, k * D:(k + 1) * D].rearrange("p (h d) -> p h d", d=HD))
                last.then_inc(v1_ready, 1)
            for n in range(2):
                act.wait_ge(r1_ready, n + 1)
                for k in range(2):
                    last = copy(v_part[:, 2 * n + k, 0:HEADS, 1, 0:HD],
                                v_rest[:, 2 * n + k].rearrange("p (h d) -> p h d", d=HD))
                last.then_inc(v2_ready, 1)
            normalise(1, 0)
            normalise(1, 1)
            rows_high(1)
            queries_high(1, 1)

            def step(g, u, scores_next, project_next):
                first = isinstance(g, int) and g == 0
                if scores_next and not first:
                    queries_high(g + 1, 1 - u)
                for j in range(C * NJ):
                    exps(g, j)
                    if j == 0 and not first:
                        heads_transposed(g - 1)
                    if project_next and j in (4, 6):
                        normalise(g + 2, (j - 4) // 2)
                if project_next:
                    rows_high(g + 2)
                if isinstance(g, int) and g < 2:
                    keys_high(g + 1)
                    if g == 1:
                        keys_high(3)

            for g in range(2):
                step(g, g, True, True)
            with act.Fori(2, NG - 3, 2) as r:
                for u in range(2):
                    step(r + u, u, True, True)
            step(NG - 2, 0, True, False)
            step(NG - 1, 1, False, False)
            heads_transposed(NG - 1)

        @block.vector
        def _(dve):
            v_ = nc.vector

            def masks(g, u):
                if not (isinstance(g, int) and g < 2):
                    dve.wait_ge(sc_filled, C * NJ * (g - 1))
                v_.tensor_scalar(mbias[:, u].rearrange("p i k -> p (i k)"),
                                 mk_raw[:, bass.ds(g, 1)].rearrange("p o k -> p (o k)"),
                                 MASKED, None, ALU.mult).then_inc(mask_ready, 1)
                v_.tensor_scalar(rhs_mm[0:KEYS, u], mt_raw[:, bass.ds(g, 1)].rearrange("p o k -> p (o k)"),
                                 MASKED, None, ALU.mult).then_inc(mask_ready, 1)

            def nans(g, u):
                v_.tensor_scalar(allmasked[:], mx[:], MASKED / 2, 3e38, ALU.is_le, ALU.mult).then_inc(nan_step, 1)
                dve.wait_ge(nan_step, g + 1)
                v_.tensor_scalar(nanfix[:, u], allmasked[:], 3e38, 0.0, ALU.mult, ALU.mult).then_inc(nan_ready, 1)

            def stats_of(g):
                dve.wait_ge(x_in, (g + 1) * 16)
                for i in range(TG):
                    v_.bn_stats(stats[:, i], x_res[:, bass.ds(g * TG + i, 1), :].rearrange("p o d -> p (o d)")
                                ).then_inc(stat_step, 1)
                dve.wait_ge(stat_step, TG * (g + 1))
                v_.memset(hold[:], 0.0)
                for i in range(TG):
                    v_.bn_aggr(mv[:, i], stats[:, i]).then_inc(aggr_step, 1)
                dve.wait_ge(aggr_step, TG * (g + 1))
                v_.tensor_scalar(negm[:], mv[:, :, 0], -1.0, None, ALU.mult)
                v_.tensor_scalar(ve[:], mv[:, :, 1], EPS, None, ALU.add).then_inc(stats_ready, 1)

            def flat(ap):
                return ap.rearrange("p t c q -> p (t c q)")

            def rows_low(g):
                for k in range(2):
                    dve.wait_ge(xt_hi_ready, 2 * g + k + 1)
                    v_.tensor_tensor(flat(xnt_lo[:, 2 * k:2 * k + 2]), flat(ps_t[k][:]),
                                     f32(flat(xnt_hi[:, 2 * k:2 * k + 2])), ALU.subtract).then_inc(xt_lo_ready, 1)

            def queries_low(g, u):
                for c in range(C):
                    dve.wait_ge(q_hi_ready, C * g + c + 1)
                    v_.scalar_tensor_tensor(q_lo[:, u, c], ps_q[c][:], bq[:, c:c + 1], f32(q_hi[:, u, c]), ALU.add,
                                            ALU.subtract).then_inc(q_lo_ready, 1)

            def exp_low(g, j):
                rows = min(P, HK - (j % NJ) * P)
                dve.wait_ge(pf_ready, C * NJ * g + j + 1)
                v_.tensor_tensor(p_lo[0:rows, j], pf[0:rows, j % 2], p_hi[0:rows, j], ALU.subtract).then_inc(p_lo_ready, 1)

            def maxima(g, units):
                for n in units:
                    i, k = n // 3, n % 3
                    h0, h1 = UNITS[k]
                    dve.wait_ge(mx_filled, 3 * TG * g + n + 1)
                    v_.tensor_reduce(mx[:, i, h0:h1],
                                     ps_mx[n % 2][:, 0:(h1 - h0) * KEYS].rearrange("p (h k) -> p h k", k=KEYS),
                                     AX.X, ALU.max).then_inc(mx_used, 1)

            def maxima_parts(g, u):
                dve.wait_ge(mx_used, 3 * TG * (g + 1))
                v_.tensor_copy(mm[:, :, 0:HEADS], mx[:]).then_inc(mx_hi_step, 1)
                dve.wait_ge(mx_hi_step, g + 1)
                v_.tensor_tensor(mm[:, :, HEADS:], mx[:], f32(mm[:, :, 0:HEADS]), ALU.subtract
                                 ).then_inc(mm_ready, 1)
                nans(g, u)

            def maxima_taken(g, u):
                dve.wait_ge(mt_filled, g + 1)
                v_.tensor_copy(rhs_mm[MROW:, u], flat(ps_t[1][0:2 * HEADS])).then_inc(mt_ready, 1)

            def heads(g, u, tiles):
                dve.wait_ge(nan_ready, g + 1)
                for t in tiles:
                    num = ps_q[t % 2][:, 0:HEADS * VW].rearrange("p (h v) -> p h v", v=VW)
                    dve.wait_ge(pv_filled, TG * g + t + 1)
                    v_.tensor_tensor(den[:, t], num[:, :, HD], nanfix[:, u, t], ALU.add).then_inc(den_step, 1)
                    dve.wait_ge(den_step, TG * g + t + 1)
                    v_.reciprocal(rden[:, t], den[:, t]).then_inc(rden_step, 1)
                    dve.wait_ge(rden_step, TG * g + t + 1)
                    v_.tensor_tensor(o[:, t].rearrange("p (h d) -> p h d", d=HD), num[:, :, 0:HD],
                                     rden[:, t].unsqueeze(2).to_broadcast([P, HEADS, HD]), ALU.mult).then_inc(o_ready, 1)

            def residual(g, t):
                dve.wait_ge(op_filled, TG * g + t + 1)
                dve.wait_ge(xb_ready, TG * (g + 1))
                at = x_res[:, bass.ds(g * TG + t, 1), :].rearrange("p o d -> p (o d)")
                v_.tensor_tensor(at, ps_q[t % 2][:, 0:D], at, ALU.add).then_inc(x1_ready, 1)

            def heads_transposed(g, k):
                dve.wait_ge(ot_hi_ready, 2 * g + k + 1)
                v_.tensor_tensor(flat(ot_lo[:, 2 * k:2 * k + 2]), flat(ps_t[k][:]),
                                 f32(flat(ot_hi[:, 2 * k:2 * k + 2])), ALU.subtract).then_inc(ot_lo_ready, 1)

            def keys_of(b):
                for c in range(C):
                    last = v_.tensor_tensor(kb[:, c], kt[:, c, b].unsqueeze(1).to_broadcast([P, HC, KEYS]),
                                            ksel[:].unsqueeze(2).to_broadcast([P, HC, KEYS]), ALU.mult)
                last.then_inc(kb_raw_done, 1)
                dve.wait_ge(kb_hi_done, b + 2 if b else 1)
                dst = kb_part if b else kcur
                v_.tensor_tensor(dst[:, 1], kb[:].rearrange("p c h k -> p c (h k)"), f32(dst[:, 0]), ALU.subtract
                                 ).then_inc(kb_lo_done, 1)
                dve.wait_ge(kb_hi_done, b + 2)
                dve.wait_ge(kb_lo_done, b + 1)

            def values_of(b):
                for c in range(C):
                    for k, (j0, j1) in enumerate(((0, 3), (3, NJ))):
                        dve.wait_ge(vb_mm, 4 * b + 2 * c + k + 1)
                        n = j1 - j0
                        v_.tensor_tensor(vb[:, b, c, j0:j1].rearrange("p j h k v -> p j h (k v)"),
                                         ps_q[k][:, 0:n * NHMAX * 3 * VW].rearrange("p (j h w) -> p j h w", j=n, h=NHMAX),
                                         vmask[:, j0:j1].unsqueeze(3).to_broadcast([P, n, NHMAX, 3 * VW]), ALU.mult
                                         ).then_inc(vb_done, 1)

            v_.memset(f32(rhs_mm[64:P]), 0.0).then_inc(rhs_zeroed, 1)
            stats_of(0)
            for c in range(C):
                dve.wait_ge(kt_mm, c + 1)
                v_.tensor_scalar(kt[:, c].rearrange("p b k -> p (b k)"), ps_sc[c][:, 0:B * KEYS], bk[:, c:c + 1], None,
                                 ALU.add).then_inc(kt_ready, 1)
            for n, i in ((0, Q), (1, O)):
                dve.wait_ge(w_hi_ready, n + 1)
                v_.tensor_tensor(w_lo[:, n], w_raw[:, i], f32(w_hi[:, n]), ALU.subtract).then_inc(w_lo_ready, 1)
            dve.wait_ge(kt_ready, C)
            dve.wait_ge(const_in, NCONST)
            keys_of(0)
            dve.wait_ge(mask_in, 32)
            masks(0, 0)
            masks(1, 1)
            rows_low(0)
            queries_low(0, 0)
            stats_of(1)
            for n in range(2):
                dve.wait_ge(v1_ready, n + 1)
                for k in range(2):
                    last = v_.tensor_tensor(v_rest[:, 2 * n + k].rearrange("p (h d) -> p h d", d=HD),
                                            ps_mx[n][0:KEYS, k * D:(k + 1) * D].rearrange("p (h d) -> p h d", d=HD),
                                            v_part[:, 2 * n + k, 0:HEADS, 0, 0:HD], ALU.subtract)
                last.then_inc(r1_ready, 1)
            for n in range(2):
                dve.wait_ge(v2_ready, n + 1)
                for k in range(2):
                    last = v_.tensor_tensor(v_part[:, 2 * n + k, 0:HEADS, 2, 0:HD],
                                            v_rest[:, 2 * n + k].rearrange("p (h d) -> p h d", d=HD),
                                            v_part[:, 2 * n + k, 0:HEADS, 1, 0:HD], ALU.subtract)
                last.then_inc(v3_ready, 1)
            values_of(0)
            maxima(0, range(3 * TG))
            maxima_parts(0, 0)
            maxima_taken(0, 0)
            rows_low(1)
            queries_low(1, 1)

            def step(g, u, scores_next, project_next):
                first = isinstance(g, int) and g == 0
                if scores_next and not first:
                    queries_low(g + 1, 1 - u)
                for j in range(C * NJ):
                    if scores_next and j:
                        maxima(g + 1, range(QUOTA[j - 1], QUOTA[j]))
                    exp_low(g, j)
                    if j == 0 and not first:
                        for k in range(2):
                            heads_transposed(g - 1, k)
                    if project_next and j == 1:
                        stats_of(g + 2)
                    if not first and 3 <= j < 3 + TG:
                        residual(g - 1, j - 3)
                if scores_next:
                    maxima_parts(g + 1, 1 - u)
                if project_next:
                    rows_low(g + 2)
                heads(g, u, (0, 1))
                if scores_next:
                    maxima_taken(g + 1, 1 - u)
                heads(g, u, (2, 3))
                if project_next:
                    masks(g + 2, u)
                if isinstance(g, int) and g < 2:
                    keys_of(g + 1)
                    values_of(g + 1)
                    if g == 1:
                        keys_of(3)
                        values_of(3)

            for g in range(2):
                step(g, g, True, True)
            with dve.Fori(2, NG - 3, 2) as r:
                for u in range(2):
                    step(r + u, u, True, True)
            step(NG - 2, 0, True, False)
            step(NG - 1, 1, False, False)
            for k in range(2):
                heads_transposed(NG - 1, k)
            for t in range(TG):
                residual(NG - 1, t)

        @block.tensor
        def _(pe):
            mm_ = nc.tensor.matmul

            def transposed(bank, rows):
                for k in range(2):
                    for c in range(C):
                        last = nc.tensor.transpose(bank[:, k, c], rows[:, k, c * P:(c + 1) * P], ident[:])
                return last

            def split_product(dst, pairs):
                todo = [(l, r) for lh, ll, rh, rl in pairs for l, r in ((lh, rh), (ll, rh), (lh, rl))]
                for n, (l, r) in enumerate(todo):
                    last = mm_(dst, l, r, start=(n == 0), stop=(n == len(todo) - 1))
                return last

            def rows_transposed(g):
                for k in range(2):
                    pe.wait_ge(xn_ready, 2 * g + k + 1)
                    if k == 1 and isinstance(g, int) and g == 1:
                        pe.wait_ge(mt_ready, 1)
                    transposed(ps_t[k], xn[:, 2 * k:2 * k + 2]).then_inc(xt_filled, 1)

            def queries(g):
                pe.wait_ge(xt_lo_ready, 2 * g + 2)
                for c in range(C):
                    if not (isinstance(g, int) and g < 2):
                        pe.wait_ge(o_ready, TG * (g - 2) + 3 + c)
                    split_product(ps_q[c][:], [(w_hi[:, 0, k, c * P:(c + 1) * P], w_lo[:, 0, k, c * P:(c + 1) * P],
                                                xnt_hi[:, :, k, :], xnt_lo[:, :, k, :]) for k in range(C)]
                                  ).then_inc(q_filled, 1)

            def values_of(b):
                for c in range(C):
                    for k, (j0, j1) in enumerate(((0, 3), (3, NJ))):
                        if 4 * b + 2 * c + k >= 2:
                            pe.wait_ge(vb_done, 4 * b + 2 * c + k - 1)
                        for j in range(j0, j1):
                            at = c * HC + TILE_HEADS[j][0]
                            w = NHMAX * 3 * VW
                            last = mm_(ps_q[k][:, (j - j0) * w:(j - j0 + 1) * w], sel_b[:, c, j * P:(j + 1) * P],
                                       v_part[:, b, at:at + NHMAX].rearrange("p h k v -> p (h k v)"), start=True, stop=True)
                        last.then_inc(vb_mm, 1)

            pe.wait_ge(wattn_in, NATTN)
            for c in range(C):
                for k in range(C):
                    last = mm_(ps_sc[c][:, 0:B * KEYS], w_raw[:, K, k, c * P:(c + 1) * P], ctx_t[:, k],
                               start=(k == 0), stop=(k == C - 1))
                last.then_inc(kt_mm, 1)
            pe.wait_ge(zeroed, 4)
            for b in range(B):
                dst = ps_mx[b // 2][0:KEYS, (b % 2) * D:(b % 2 + 1) * D]
                for k in range(C):
                    mm_(dst, ctx_t[:, k, b * KEYS:(b + 1) * KEYS], w_raw[:, V, k], start=(k == 0), stop=False)
                last = mm_(dst, ones1[0:1, 0:KEYS], bv[0:1, :], start=False, stop=True)
                if b % 2:
                    last.then_inc(v_mm, 1)
            pe.wait_ge(const_in, NCONST)
            pe.wait_ge(w_lo_ready, 2)

            def maxima(g, u, n):
                i, k = n // 3, n % 3
                h0, h1 = UNITS[k]
                bank = ps_mx[n % 2]
                mm_(bank[:, 0:(h1 - h0) * KEYS], ident_b[:],
                    mbias[:, u, i].unsqueeze(1).to_broadcast([P, h1 - h0, KEYS]), start=True, stop=True)
                for c in range(C):
                    lo, hi = max(h0, c * HC), min(h1, (c + 1) * HC)
                    if lo < hi:
                        last = mm_(bank[:, (lo - h0) * KEYS:(hi - h0) * KEYS], q_hi[:, u, c, i * P:(i + 1) * P],
                                   kmax[:, c, (lo - c * HC) * KEYS:(hi - c * HC) * KEYS],
                                   start=False, stop=True, skip_group_check=True)
                last.then_inc(mx_filled, 1)

            def maxima_begin(g):
                pe.wait_ge(q_hi_ready, C * (g + 1))
                pe.wait_ge(mask_ready, 2 * (g + 1))
                if isinstance(g, int) and g < 2:
                    pe.wait_ge(kb_hi_done, 2)
                else:
                    pe.wait_ge(kmax_in, (g // 2) * 16)

            def maxima_transposed(g):
                pe.wait_ge(mm_ready, g + 1)
                for i in range(TG):
                    last = nc.tensor.transpose(ps_t[1][0:2 * HEADS, i // 2, i % 2], f32(mm[:, i]), ident[:])
                last.then_inc(mt_filled, 1)

            def scores(g, u, n):
                c, j = divmod(n, NJ)
                rows = min(P, HK - j * P)
                dst = ps_sc[n % 2][0:rows]
                at = slice(j * P, j * P + rows)
                mm_(dst, sel_r[:, c, at], rhs_mm[:, u], start=True, stop=False)
                mm_(dst, kcur[:, 0, c, at], q_hi[:, u, c], start=False, stop=False)
                mm_(dst, kcur[:, 1, c, at], q_hi[:, u, c], start=False, stop=False)
                mm_(dst, kcur[:, 0, c, at], q_lo[:, u, c], start=False, stop=True).then_inc(sc_filled, 1)

            def values(g, t):
                if t >= 2:
                    pe.wait_ge(o_ready, TG * g + t - 1)
                for n in range(C * NJ):
                    c, j = divmod(n, NJ)
                    rows = min(P, HK - j * P)
                    h0, nh = TILE_HEADS[j]
                    dst = ps_q[t % 2][:, (c * HC + h0) * VW:(c * HC + h0 + nh) * VW]
                    for i, (p, part) in enumerate(((p_hi, 0), (p_hi, 1), (p_hi, 2), (p_lo, 0), (p_lo, 1))):
                        last = mm_(dst, p[0:rows, n, t * P:(t + 1) * P],
                                   vb[0:rows, bass.ds(g // 2, 1), c, j, 0:nh, part, :].rearrange("p o h v -> p (o h) v"),
                                   start=(n == 0 and i == 0), stop=True, skip_group_check=True)
                last.then_inc(pv_filled, 1)

            def heads_transposed(g, k):
                pe.wait_ge(o_ready, TG * g + 2 * k + 2)
                transposed(ps_t[k], o[:, 2 * k:2 * k + 2]).then_inc(ot_filled, 1)

            def out_projection(g, t):
                pe.wait_ge(ot_lo_ready, 2 * g + t // 2 + 1)
                if t >= 2:
                    pe.wait_ge(x1_ready, TG * g + t - 1)
                split_product(ps_q[t % 2][:, 0:D], [(ot_hi[:, t, k], ot_lo[:, t, k], w_hi[:, 1, k], w_lo[:, 1, k])
                                                    for k in range(C)]).then_inc(op_filled, 1)

            rows_transposed(0)
            queries(0)
            pe.wait_ge(consts_ready, 3)
            pe.wait_ge(rhs_zeroed, 1)
            pe.wait_ge(v3_ready, 2)
            pe.wait_ge(q_lo_ready, C)
            values_of(0)
            maxima_begin(0)
            for n in range(3 * TG):
                if n >= 2:
                    pe.wait_ge(mx_used, n - 1)
                maxima(0, 0, n)
            maxima_transposed(0)
            pe.wait_ge(vb_done, 4)
            rows_transposed(1)
            queries(1)
            pe.wait_ge(q_lo_ready, 2 * C)

            def step(g, u, scores_next, project_next):
                first = isinstance(g, int) and g == 0
                pe.wait_ge(mt_ready, g + 1)
                if not (isinstance(g, int) and g < 2):
                    pe.wait_ge(kcur_in, (g // 2) * 16)
                else:
                    pe.wait_ge(kb_lo_done, 1)
                for n in range(C * NJ):
                    if not (first and n < 2):
                        pe.wait_ge(pf_ready, C * NJ * g + n - 1)
                    scores(g, u, n)
                    if n == 0 and not first:
                        for k in range(2):
                            heads_transposed(g - 1, k)
                    if scores_next and n:
                        if n == 1:
                            maxima_begin(g + 1)
                        for unit in range(QUOTA[n - 1], QUOTA[n]):
                            pe.wait_ge(mx_used, 3 * TG * (g + 1) + unit - 1)
                            maxima(g + 1, 1 - u, unit)
                    if not first and 2 <= n < 2 + TG:
                        if scores_next and n == 2:
                            pe.wait_ge(q_lo_ready, C * (g + 2))
                        out_projection(g - 1, n - 2)
                if project_next:
                    rows_transposed(g + 2)
                pe.wait_ge(p_lo_ready, C * NJ * (g + 1))
                if not first:
                    pe.wait_ge(x1_ready, TG * g)
                for t in range(TG):
                    values(g, t)
                    if t == 1 and scores_next:
                        if project_next:
                            pe.wait_ge(xt_lo_ready, 2 * g + 6)
                        maxima_transposed(g + 1)
                if isinstance(g, int) and g < 2:
                    pe.wait_ge(o_ready, TG * (g + 1))
                    values_of(g + 1)
                    if g == 1:
                        values_of(3)
                    pe.wait_ge(vb_done, 4 * (g + 2 if g == 0 else 4))
                if project_next:
                    queries(g + 2)

            for g in range(2):
                step(g, g, True, True)
            with pe.Fori(2, NG - 3, 2) as r:
                for u in range(2):
                    step(r + u, u, True, True)
            step(NG - 2, 0, True, False)
            step(NG - 1, 1, False, False)
            for k in range(2):
                heads_transposed(NG - 1, k)
            for t in range(TG):
                out_projection(NG - 1, t)


def feed_forward(nc, a, out, x_res, ident):
    ctx = ExitStack()
    with ctx:
        def sb(name, shape, dt=F32):
            return ctx.enter_context(nc.sbuf_tensor(name, shape, dt))

        def ps(name, shape, dt=F32):
            return ctx.enter_context(nc.psum_tensor(name, shape, dt))

        def sem(name):
            return ctx.enter_context(nc.semaphore(name))

        def f32(ap):
            return ap.bitcast(F32)

        ORDER = [E, E + 1] + list(range(E))
        NU = len(ORDER)
        NRAW = 3
        STEPS = 20
        gu_hi = sb("gu_hi", [P, C, NU, 2 * DE], F32R)
        gu_lo = sb("gu_lo", [P, C, NU, 2 * DE], F32R)
        dn_hi = sb("dn_hi", [P, NU, D], F32R)
        dn_lo = sb("dn_lo", [P, NU, D], F32R)
        raw = sb("raw", [P, NRAW, C + 1, 2 * DE])
        r_raw = sb("r_raw", [P, C, E])
        r_part = sb("r_part", [P, C, 2 * E], F32R)
        x2_hi = sb("x2_hi", [P, 2, TG, C, P], F32R)
        x2_lo = sb("x2_lo", [P, 2, TG, C, P], F32R)
        stats = sb("stats2", [P, TG, 6])
        mv = sb("mv2", [P, TG, 2])
        ve = sb("ve2", [P, TG])
        rstd = sb("rstd2", [P, TG])
        pow_e = sb("pow_e2", [P, TG])
        hold = sb("hold2", [P, 1])
        negm = sb("negm", [P, TG])
        xc = sb("xc", [P, TG, D])
        xn = sb("xn2", [P, TG, D])
        rt = sb("rt", [P, GT])
        lparts = sb("lparts", [P, TG, 2 * E])
        logit = sb("logit", [P, TG, E])
        iota = sb("iota", [P, TG, E])
        work = sb("work", [P, TG, E])
        prob = sb("prob", [P, TG, E])
        one1 = sb("one1", [P, TG, E])
        one2 = sb("one2", [P, TG, E])
        coef = sb("coef", [P, 2, TG, E])
        top = sb("top", [P, TG])
        at1 = sb("at1", [P, TG])
        rsum = sb("rsum", [P, TG])
        sg = sb("sg", [P, 2, GT])
        hid = sb("hid", [P, 2, GT])
        h_hi = sb("h_hi", [P, 2, GT], F32R)
        h_lo = sb("h_lo", [P, 2, GT], F32R)

        ps_g = [ps(f"ps_g{i}", [P, GT]) for i in range(2)]
        ps_u = [ps(f"ps_u{i}", [P, GT]) for i in range(2)]
        ps_y = [ps(f"ps_y{i}", [P, 2, D]) for i in range(2)]
        ps_r = [ps(f"ps_r{i}", [P, 2, C, P]) for i in range(2)]

        w_in = [sem(f"w_in{i}") for i in range(NRAW)]
        r_in = sem("r_in")
        w_hi_ready = sem("fw_hi_ready")
        w_lo_ready = sem("fw_lo_ready")
        r_hi_ready = sem("r_hi_ready")
        r_lo_ready = sem("r_lo_ready")
        pow_ready = sem("pow_ready")
        rt_zeroed = sem("rt_zeroed")
        stat_step = sem("f_stat_step")
        aggr_step = sem("f_aggr_step")
        stats_ready = sem("f_stats_ready")
        rstd_ready = sem("f_rstd_ready")
        xc_ready = sem("xc_ready")
        xn_ready = sem("f_xn_ready")
        xt_filled = sem("f_xt_filled")
        x2_hi_ready = sem("x2_hi_ready")
        x2_lo_ready = sem("x2_lo_ready")
        rt_filled = sem("rt_filled")
        rt_ready = sem("rt_ready")
        lg_filled = sem("lg_filled")
        iota_ready = sem("iota_ready")
        route_step = sem("route_step")
        shifted = sem("shifted")
        exped = sem("exped")
        gate_filled = sem("gate_filled")
        up_filled = sem("up_filled")
        silu_ready = sem("silu_ready")
        h_ready = sem("h_ready")
        h_hi_ready = sem("h_hi_ready")
        h_lo_ready = sem("h_lo_ready")
        y_filled = sem("y_filled")
        y_used = sem("y_used")
        out_done = sem("out_done")

        out_v = out.rearrange("b (g p i) d -> (b g) p i d", p=P, i=TG)
        block = ctx.enter_context(nc.Block())

        @block.sync
        def _(sp):
            sp.dma_start(r_raw[:], a["router"].rearrange("(c p) e -> p c e", p=P)).then_inc(r_in, 16)
            for n, e in enumerate(ORDER):
                s = n % NRAW
                if n >= NRAW:
                    sp.wait_ge(w_lo_ready, 2 * (n - NRAW + 1))
                if e < E:
                    gate, up, down = a["eg"][e], a["eu"][e], a["ed"][e]
                else:
                    at = slice((e - E) * DE, (e - E + 1) * DE)
                    gate, up, down = a["sgate"][:, at], a["sup"][:, at], a["sdown"][at, :]
                sp.dma_start(raw[:, s, 0:C, 0:DE], gate.rearrange("(c p) d -> p c d", p=P)).then_inc(w_in[s], 16)
                sp.dma_start(raw[:, s, 0:C, DE:], up.rearrange("(c p) d -> p c d", p=P)).then_inc(w_in[s], 16)
                sp.dma_start(raw[:, s, C, :], down).then_inc(w_in[s], 16)
            for g in range(NG):
                sp.wait_ge(y_used, 2 * (NU - 1) * (g + 1))
                sp.dma_start(out_v[g], x_res[:, g * TG:(g + 1) * TG, :]).then_inc(out_done, 16)
            sp.wait_ge(out_done, 16 * NG)

        @block.gpsimd
        def _(pool):
            g_ = nc.gpsimd
            g_.memset(pow_e[:], -0.5).then_inc(pow_ready, 1)
            g_.iota(iota[:], [[0, TG], [1, E]], base=-E, channel_multiplier=0,
                    allow_small_or_imprecise_dtypes=True).then_inc(iota_ready, 1)
            g_.memset(rt[:], 0.0).then_inc(rt_zeroed, 1)
            pool.wait_ge(pow_ready, 1)

            def norm(g):
                pool.wait_ge(stats_ready, g + 1)
                g_.tensor_tensor(rstd[:], ve[:], pow_e[:], ALU.pow).then_inc(rstd_ready, 1)

            norm(0)
            with pool.Fori(1, NG) as g:
                norm(g)

        @block.scalar
        def _(act):
            def copy(dst, src):
                return nc.scalar.activation(dst, src, ACT.Copy)

            def split(n):
                act.wait_ge(w_in[n % NRAW], 48 * (n // NRAW + 1))
                copy(gu_hi[:, :, n], raw[:, n % NRAW, 0:C]).then_inc(w_hi_ready, 1)
                copy(dn_hi[:, n], raw[:, n % NRAW, C]).then_inc(w_hi_ready, 1)

            def normalise(g, tiles):
                if tiles[0] == 0:
                    act.wait_ge(rstd_ready, g + 1)
                    if not (isinstance(g, int) and g == 0):
                        act.wait_ge(xt_filled, 2 * g)
                for i in range(*tiles):
                    at = x_res[:, bass.ds(g * TG + i, 1), :].rearrange("p o d -> p (o d)")
                    last = nc.scalar.activation(xc[:, i], at, ACT.Identity, bias=negm[:, i:i + 1])
                last.then_inc(xc_ready, 1)
                act.wait_ge(xc_ready, 2 * g + tiles[1] // 2)
                for i in range(*tiles):
                    last = nc.scalar.activation(xn[:, i], xc[:, i], ACT.Copy, scale=rstd[:, i:i + 1])
                last.then_inc(xn_ready, 1)

            def rows_high(g, u, k):
                act.wait_ge(xt_filled, 2 * g + k + 1)
                copy(x2_hi[:, u, 2 * k:2 * k + 2], ps_r[k][:]).then_inc(x2_hi_ready, 1)

            def logits(g):
                act.wait_ge(rt_filled, g + 1)
                copy(rt[0:2 * E], ps_r[0][0:2 * E].rearrange("p t c q -> p (t c q)")).then_inc(rt_ready, 1)

            def exps(g):
                act.wait_ge(shifted, g + 1)
                nc.scalar.activation(prob[:], work[:], ACT.Exp).then_inc(exped, 1)

            def silu(n, b):
                act.wait_ge(gate_filled, n + 1)
                nc.scalar.activation(sg[:, b], ps_g[b][:], ACT.Silu).then_inc(silu_ready, 1)

            def hidden_high(n, b):
                act.wait_ge(h_ready, n + 1)
                copy(h_hi[:, b], hid[:, b]).then_inc(h_hi_ready, 1)

            def group(g, u, more):
                for m in range(NU):
                    n, b = NU * g + m, m % 2
                    silu(n, b)
                    hidden_high(n, b)
                    if isinstance(g, int) and g == 0 and m + 2 < NU:
                        split(m + 2)
                    if more and m in (1, 2):
                        normalise(g + 1, (2 * m - 2, 2 * m))
                    if more and m in (3, 4):
                        rows_high(g + 1, 1 - u, m - 3)
                    if more and m == 6:
                        logits(g + 1)
                    if more and m == NU - 1:
                        exps(g + 1)

            normalise(0, (0, 2))
            normalise(0, (2, 4))
            act.wait_ge(r_in, 16)
            copy(r_part[:, :, 0:E], r_raw[:]).then_inc(r_hi_ready, 1)
            rows_high(0, 0, 0)
            rows_high(0, 0, 1)
            act.wait_ge(rt_zeroed, 1)
            logits(0)
            split(0)
            split(1)
            exps(0)
            group(0, 0, True)
            with act.Fori(1, NG - 2, 2) as r:
                group(r, 1, True)
                group(r + 1, 0, True)
            group(NG - 1, 1, False)

        @block.vector
        def _(dve):
            v_ = nc.vector

            def flat(ap):
                return ap.rearrange("p t c q -> p (t c q)")

            def split(n):
                dve.wait_ge(w_hi_ready, 2 * n + 2)
                v_.tensor_tensor(gu_lo[:, :, n], raw[:, n % NRAW, 0:C], f32(gu_hi[:, :, n]), ALU.subtract).then_inc(w_lo_ready, 1)
                v_.tensor_tensor(dn_lo[:, n], raw[:, n % NRAW, C], f32(dn_hi[:, n]), ALU.subtract).then_inc(w_lo_ready, 1)

            def row(g, i):
                return x_res[:, bass.ds(g * TG + i, 1), :].rearrange("p o d -> p (o d)")

            def stats_of(g):
                for i in range(TG):
                    v_.bn_stats(stats[:, i], row(g, i)).then_inc(stat_step, 1)
                dve.wait_ge(stat_step, TG * (g + 1))
                v_.memset(hold[:], 0.0)
                for i in range(TG):
                    v_.bn_aggr(mv[:, i], stats[:, i]).then_inc(aggr_step, 1)
                dve.wait_ge(aggr_step, TG * (g + 1))
                v_.tensor_scalar(negm[:], mv[:, :, 0], -1.0, None, ALU.mult)
                v_.tensor_scalar(ve[:], mv[:, :, 1], EPS, None, ALU.add).then_inc(stats_ready, 1)

            def rows_low(g, u, k):
                dve.wait_ge(x2_hi_ready, 2 * g + k + 1)
                v_.tensor_tensor(flat(x2_lo[:, u, 2 * k:2 * k + 2]), flat(ps_r[k][:]),
                                 f32(flat(x2_hi[:, u, 2 * k:2 * k + 2])), ALU.subtract).then_inc(x2_lo_ready, 1)

            steps = [0]

            def link(g, ins):
                steps[0] += 1
                ins.then_inc(route_step, 1)
                dve.wait_ge(route_step, STEPS * g + steps[0])

            def spread(ap):
                return ap.unsqueeze(2).to_broadcast([P, TG, E])

            def choose(g, values, one):
                link(g, v_.tensor_reduce(top[:], values, AX.X, ALU.max))
                link(g, v_.tensor_tensor(one, values, spread(top[:]), ALU.is_equal))
                link(g, v_.scalar_tensor_tensor(one, one, -float(E), iota[:], ALU.mult, ALU.add))
                link(g, v_.tensor_reduce(at1[:], one, AX.X, ALU.min))
                link(g, v_.tensor_scalar(at1[:], at1[:], -float(E) - 1.0, float(E), ALU.min, ALU.add))
                link(g, v_.tensor_tensor(one, iota[:], spread(at1[:]), ALU.is_equal))

            def route_first(g):
                steps[0] = 0
                dve.wait_ge(lg_filled, g + 1)
                link(g, v_.tensor_copy(lparts[:], flat(ps_r[1][:]).rearrange("p (t e) -> p t e", e=P)[:, :, 0:2 * E]))
                link(g, v_.tensor_tensor(logit[:], lparts[:, :, 0:E], lparts[:, :, E:], ALU.add))
                choose(g, logit[:], one1[:])
                v_.tensor_tensor(work[:], logit[:], spread(top[:]), ALU.subtract).then_inc(shifted, 1)
                link(g, v_.scalar_tensor_tensor(one2[:], one1[:], -3e38, logit[:], ALU.mult, ALU.add))

            def route_second(g):
                link(g, v_.tensor_copy(logit[:], one2[:]))
                choose(g, logit[:], one2[:])

            def route_coef(g, u):
                dve.wait_ge(exped, g + 1)
                link(g, v_.tensor_reduce(rsum[:], prob[:], AX.X, ALU.add))
                link(g, v_.reciprocal(rsum[:], rsum[:]))
                link(g, v_.tensor_tensor(prob[:], prob[:], spread(rsum[:]), ALU.mult))
                link(g, v_.tensor_tensor(one1[:], one1[:], one2[:], ALU.add))
                v_.tensor_tensor(coef[:, u], one1[:], prob[:], ALU.mult)

            def hidden(n, b):
                dve.wait_ge(silu_ready, n + 1)
                dve.wait_ge(up_filled, n + 1)
                v_.tensor_tensor(hid[:, b], sg[:, b], ps_u[b][:], ALU.mult).then_inc(h_ready, 1)

            def hidden_low(n, b):
                dve.wait_ge(h_hi_ready, n + 1)
                v_.tensor_tensor(h_lo[:, b], hid[:, b], f32(h_hi[:, b]), ALU.subtract).then_inc(h_lo_ready, 1)

            def add(g, u, m):
                n = (NU - 1) * g + m - 1
                if not (isinstance(n, int) and n == 0):
                    dve.wait_ge(y_used, 2 * n)
                for k in range(2):
                    dve.wait_ge(y_filled, 2 * n + k + 1)
                    for i in range(2):
                        t = 2 * k + i
                        weight = 1.0 if ORDER[m] >= E else coef[:, u, t, ORDER[m]:ORDER[m] + 1]
                        last = v_.scalar_tensor_tensor(row(g, t), ps_y[k][:, i], weight, row(g, t), ALU.mult, ALU.add)
                    last.then_inc(y_used, 1)

            def group(g, u, more):
                first = isinstance(g, int) and g == 0
                for m in range(NU):
                    n, b = NU * g + m, m % 2
                    hidden(n, b)
                    if m > 1:
                        add(g, u, m - 1)
                    elif m == 0 and not first:
                        add(g - 1, 1 - u, NU - 1)
                    hidden_low(n, b)
                    if first and m + 2 < NU:
                        split(m + 2)
                    if m == 0 and not first:
                        route_coef(g, u)
                    if more:
                        if m == 0:
                            stats_of(g + 1)
                        if m in (3, 4):
                            rows_low(g + 1, 1 - u, m - 3)
                        if m == 8:
                            route_first(g + 1)
                        if m == 9:
                            route_second(g + 1)

            stats_of(0)
            dve.wait_ge(r_hi_ready, 1)
            v_.tensor_tensor(r_part[:, :, E:], r_raw[:], f32(r_part[:, :, 0:E]), ALU.subtract).then_inc(r_lo_ready, 1)
            rows_low(0, 0, 0)
            rows_low(0, 0, 1)
            split(0)
            split(1)
            dve.wait_ge(iota_ready, 1)
            route_first(0)
            route_second(0)
            route_coef(0, 0)
            group(0, 0, True)
            with dve.Fori(1, NG - 2, 2) as r:
                group(r, 1, True)
                group(r + 1, 0, True)
            group(NG - 1, 1, False)
            add(NG - 1, 1, NU - 1)

        @block.tensor
        def _(pe):
            mm_ = nc.tensor.matmul

            def transposed(g, k):
                pe.wait_ge(xn_ready, 2 * g + k + 1)
                if not (isinstance(g, int) and g == 0):
                    if k == 0:
                        pe.wait_ge(rt_ready, g)
                    else:
                        pe.wait_ge(route_step, STEPS * (g - 1) + 1)
                for i in range(2):
                    for c in range(C):
                        last = nc.tensor.transpose(ps_r[k][:, i, c], xn[:, 2 * k + i, c * P:(c + 1) * P], ident[:])
                last.then_inc(xt_filled, 1)

            def logits(g, u):
                pe.wait_ge(x2_lo_ready, 2 * g + 2)
                dst = ps_r[0][0:2 * E].rearrange("p t c q -> p (t c q)")
                i = 0
                for k in range(C):
                    for x in (x2_hi, x2_lo):
                        last = mm_(dst, r_part[:, k], x[:, u, :, k], start=(i == 0), stop=(i == 2 * C - 1))
                        i += 1
                last.then_inc(rt_filled, 1)

            def logits_transposed(g):
                pe.wait_ge(rt_ready, g + 1)
                for i in range(TG):
                    last = nc.tensor.transpose(ps_r[1][:, i // 2, i % 2], rt[:, i * P:(i + 1) * P], ident[:])
                last.then_inc(lg_filled, 1)

            def gate_up(n, u, b, m):
                if not isinstance(n, int) or n >= 2:
                    pe.wait_ge(h_ready, n - 1)
                for bank, at, filled in ((ps_g[b], 0, gate_filled), (ps_u[b], DE, up_filled)):
                    i = 0
                    for k in range(C):
                        for w, x in ((gu_hi, x2_hi), (gu_lo, x2_hi), (gu_hi, x2_lo)):
                            last = mm_(bank[:], w[:, k, m, at:at + DE], x[:, u, :, k], start=(i == 0), stop=(i == 3 * C - 1))
                            i += 1
                    last.then_inc(filled, 1)

            def down(n, g, b, m):
                pe.wait_ge(h_lo_ready, n + 1)
                for k in range(2):
                    if m != 1 and not (isinstance(g, int) and g == 0 and m == 0):
                        pe.wait_ge(y_used, 2 * ((NU - 1) * g + max(m - 1, 0) - 1) + k + 1)
                    for i in range(2):
                        at = slice((2 * k + i) * P, (2 * k + i + 1) * P)
                        for j, (h, w) in enumerate(((h_hi, dn_hi), (h_lo, dn_hi), (h_hi, dn_lo))):
                            last = mm_(ps_y[k][:, i], h[:, b, at], w[:, m], start=(m != 1 and j == 0 and (m > 0 or i == 0)),
                                       stop=(j == 2 or m < 2), skip_group_check=(m < 2))
                    if m > 0:
                        last.then_inc(y_filled, 1)

            def group(g, u, more):
                first = isinstance(g, int) and g == 0
                pe.wait_ge(x2_lo_ready, 2 * g + 2)
                for m in range(NU):
                    n, b = NU * g + m, m % 2
                    if first:
                        pe.wait_ge(w_lo_ready, 2 * (m + 1))
                    gate_up(n, u, b, m)
                    if not (first and m == 0):
                        down(n - 1, g if m else g - 1, 1 - b, (m - 1) % NU)
                    if more:
                        if m in (2, 3):
                            transposed(g + 1, m - 2)
                        if m == 5:
                            logits(g + 1, 1 - u)
                        if m == 7:
                            logits_transposed(g + 1)

            transposed(0, 0)
            transposed(0, 1)
            pe.wait_ge(r_lo_ready, 1)
            logits(0, 0)
            logits_transposed(0)
            group(0, 0, True)
            with pe.Fori(1, NG - 2, 2) as r:
                group(r, 1, True)
                group(r + 1, 0, True)
            group(NG - 1, 1, False)
            down(NU * NG - 1, NG - 1, (NU - 1) % 2, NU - 1)


_NAMES = {"x": "x", "wq": "L0_xattn_wq", "wk": "L0_xattn_wk", "wv": "L0_xattn_wv", "wo": "L0_xattn_wo",
          "router": "L0_ffn_router", "eg": "L0_ffn_experts_gate", "eu": "L0_ffn_experts_up",
          "ed": "L0_ffn_experts_down", "sgate": "L0_ffn_shared_gate", "sup": "L0_ffn_shared_up",
          "sdown": "L0_ffn_shared_down"}


def kernel(**inputs):
    import concourse.bacc as _bacc
    from concourse.bass_utils import run_bass_kernel_spmd as _run

    f = {k: np.ascontiguousarray(np.asarray(v)) for k, v in inputs.items()}
    arrays = {n: f[k] for n, k in _NAMES.items()}
    arrays["ctx_t"] = np.ascontiguousarray(f["ctx_1024"].transpose(2, 0, 1).reshape(D, B * KEYS))
    for n in ("bq", "bk"):
        arrays[n] = np.ascontiguousarray(f["L0_xattn_" + n].reshape(C, P).T)
    for n in ("bv", "bo"):
        arrays[n] = f["L0_xattn_" + n].reshape(1, D)
    m = f["mask_Bx1xSxS2_bk1"].reshape(NG, P, TG, KEYS)
    arrays["mask_tok"] = m.reshape(NG, P, TG * KEYS)
    arrays["mask_key"] = np.ascontiguousarray(m.transpose(0, 3, 2, 1).reshape(NG, KEYS, GT))
    arrays.update(constants())
    nc = _bacc.Bacc("TRN2", target_bir_lowering=False, num_devices=1)
    aps = {n: nc.dram_tensor(n + "_d", v.shape, mybir.dt.from_np(v.dtype), kind="ExternalInput").ap()
           for n, v in arrays.items()}
    out = nc.dram_tensor("out_d", (B, S, D), F32, kind="ExternalOutput").ap()
    kscr = nc.dram_tensor("k_blocks", (B, P, 2 * C * HK), F32, kind="Internal").ap()
    build(nc, aps, out, kscr)
    r = _run(nc, [{n + "_d": v for n, v in arrays.items()}], core_ids=[0])
    return r.results[0]["out_d"]
```

```python
from contextlib import ExitStack

import numpy as np
import concourse.bass as bass
from concourse import mybir

F32 = mybir.dt.float32
F32R = mybir.dt.float32r
BF16 = mybir.dt.bfloat16
F16 = mybir.dt.float16
U8 = mybir.dt.uint8
ALU = mybir.AluOpType
ACT = mybir.ActivationFunctionType
AX = mybir.AxisListType

B, S, D = 4, 1024, 256
KEYS, HEADS, HD = 77, 16, 16
E, DE, DS = 8, 128, 256
P = 128
C = D // P
HC = HEADS // C
GT = 512
TG = GT // P
NG = B * S // GT
NT = B * S // P
HK = HC * KEYS
NJ = (HK + P - 1) // P
VW = HD + 1
MASKED = -(2.0 ** 120)
EPS = 1e-5
MROW = 96
HC_UNIT = 6
UNITS = [(0, 6), (6, 12), (12, 16)]
TILE_HEADS = [(P * j // KEYS, min(P * (j + 1) - 1, HK - 1) // KEYS - P * j // KEYS + 1) for j in range(NJ)]
NHMAX = max(n for _, n in TILE_HEADS)


def constants():
    f = np.arange(NJ * P)
    head, key = f // KEYS, f % KEYS
    live = f < HK
    sel = np.zeros((P, C, NJ * P), np.float32)
    for c in range(C):
        sel[key[live], c, f[live]] = 1.0
        sel[MROW + head[live] + c * HC, c, f[live]] = -1.0
        sel[MROW + HEADS + head[live] + c * HC, c, f[live]] = -1.0
    vmask = np.zeros((P, NJ, NHMAX), np.float32)
    for j, (h0, n) in enumerate(TILE_HEADS):
        for h in range(n):
            rows = f[(f // P == j) & live & (head == h0 + h)]
            vmask[rows % P, j, h] = 1.0
    ksel = np.zeros((P, HC), np.float32)
    ksel[np.arange(P), np.arange(P) // HD] = 1.0 / np.sqrt(HD)
    return {"c_sel": sel.reshape(P, -1), "c_vmask": vmask.reshape(P, -1), "c_ksel": ksel,
            "c_ident": np.eye(P, dtype=np.float32)}


ORDER = [E, E + 1] + list(range(E))
NU = len(ORDER)
NRAW = 3


class Both:

    def __init__(self, nc, ctx):
        def sb(name, shape, dt=F32):
            return ctx.enter_context(nc.sbuf_tensor(name, shape, dt))

        self.x_res = sb("x_res", [P, NT, D])
        self.ident = sb("ident", [P, P])
        self.stats = sb("stats", [P, TG, 6])
        self.mv = sb("mv", [P, TG, 2])
        self.negm = sb("negm", [P, TG])
        self.ve = sb("ve", [P, TG])
        self.rstd = sb("rstd", [P, TG])
        self.pow_e = sb("pow_e", [P, TG])
        self.hold = sb("hold", [P, 1])
        self.xc = sb("xc", [P, TG, D])
        self.xn = sb("xn", [P, TG, D])
        self.xnt_hi = sb("xnt_hi", [P, TG, C, P], F32R)
        self.xnt_lo = sb("xnt_lo", [P, TG, C, P], F32R)
        self.raw = sb("raw", [P, NRAW, C + 1, 2 * DE])
        self.r_raw = sb("r_raw", [P, C, E])
        self.w_in = [ctx.enter_context(nc.semaphore(f"w_in{i}")) for i in range(NRAW)]
        self.r_in = ctx.enter_context(nc.semaphore("r_in"))


def build(nc, a, out, kscr):
    ctx = ExitStack()
    with ctx:
        both = Both(nc, ctx)
        attention(nc, a, kscr, both)
        feed_forward(nc, a, out, both)


def load_network(sp, a, both, n):
    e, s = ORDER[n], n % NRAW
    if e < E:
        gate, up, down = a["eg"][e], a["eu"][e], a["ed"][e]
    else:
        at = slice((e - E) * DE, (e - E + 1) * DE)
        gate, up, down = a["sgate"][:, at], a["sup"][:, at], a["sdown"][at, :]
    sp.dma_start(both.raw[:, s, 0:C, 0:DE], gate.rearrange("(c p) d -> p c d", p=P)).then_inc(both.w_in[s], 16)
    sp.dma_start(both.raw[:, s, 0:C, DE:], up.rearrange("(c p) d -> p c d", p=P)).then_inc(both.w_in[s], 16)
    sp.dma_start(both.raw[:, s, C, :], down).then_inc(both.w_in[s], 16)


def attention(nc, a, kscr, both):
    x_res, ident, stats, mv, negm, ve, rstd = both.x_res, both.ident, both.stats, both.mv, both.negm, both.ve, both.rstd
    pow_e, hold, xc, xn, xnt_hi, xnt_lo = both.pow_e, both.hold, both.xc, both.xn, both.xnt_hi, both.xnt_lo
    ctx = ExitStack()
    with ctx:
        def sb(name, shape, dt=F32):
            return ctx.enter_context(nc.sbuf_tensor(name, shape, dt))

        def ps(name, shape, dt=F32):
            return ctx.enter_context(nc.psum_tensor(name, shape, dt))

        def sem(name):
            return ctx.enter_context(nc.semaphore(name))

        def f32(ap):
            return ap.bitcast(F32)

        ident_b = sb("ident_b", [P, P], BF16)
        sel_r = sb("sel_r", [P, C, NJ * P], F32R)
        sel_b = sb("sel_b", [KEYS, C, NJ * P], BF16)
        vmask = sb("vmask", [P, NJ, NHMAX])
        ksel = sb("ksel", [P, HC])
        w_raw = sb("w_raw", [P, 4, C, D])
        w_hi = sb("w_hi", [P, 2, C, D], F32R)
        w_lo = sb("w_lo", [P, 2, C, D], F32R)
        bq = sb("bq", [P, C])
        bk = sb("bk", [P, C])
        bv = sb("bv", [1, D])
        bo = sb("bo", [P, D])
        ones1 = sb("ones1", [1, P])
        warm = sb("warm", [1, P])
        ctx_t = sb("ctx_t", [P, C, B * KEYS])
        kt = sb("kt", [P, C, B, KEYS])
        v_part = sb("v_part", [KEYS, B, HEADS + 1, 3, VW], BF16)
        vcur = sb("vcur", [P, C, NJ, NHMAX, 3, VW], BF16)
        vb = sb("vb", [P, B - 1, C, NJ, NHMAX, 3, VW], BF16)
        kb = sb("kb", [P, C, HC, KEYS])
        kb_part = sb("kb_part", [P, 2, C, HK], F32R)
        NPF = 3
        kcur = sb("kcur", [P, 2, C, HK], F32R)
        kmax = sb("kmax", [P, C, HK], F32R)
        mk_raw = sb("mk_raw", [P, NG, TG * KEYS], U8)
        mt_raw = sb("mt_raw", [KEYS, NG, GT], U8)
        mbias = sb("mbias", [P, 2, TG, KEYS], BF16)
        rhs_mm = sb("rhs_mm", [P, 2, GT], F32R)
        q_hi = sb("q_hi", [P, 2, C, GT], F32R)
        q_lo = sb("q_lo", [P, 2, C, GT], F32R)
        mx = sb("mx", [P, TG, HEADS])
        mm = sb("mm", [P, TG, 2 * HEADS], F32R)
        pf = sb("pf", [P, NPF, GT])
        p_hi = sb("p_hi", [P, C * NJ, GT], F16)
        p_lo = sb("p_lo", [P, C * NJ, GT], BF16)
        allmasked = sb("allmasked", [P, TG, HEADS])
        nanfix = sb("nanfix", [P, 2, TG, HEADS])
        den = sb("den", [P, TG, HEADS])
        rden = sb("rden", [P, TG, HEADS])
        o = sb("o", [P, TG, D])
        v_rest = o[0:KEYS]
        sel_raw = p_hi[:].rearrange("p j t -> p (j t)").bitcast(F32)[:, 0:C * NJ * P]
        ot_hi = sb("ot_hi", [P, TG, C, P], F32R)
        ot_lo = sb("ot_lo", [P, TG, C, P], F32R)

        ps_mx = [ps(f"ps_mx{i}", [P, 512]) for i in range(2)]
        ps_sc = [ps(f"ps_sc{i}", [P, GT]) for i in range(2)]
        ps_t = [ps(f"ps_t{i}", [P, 2, C, P]) for i in range(2)]
        ps_q = [ps(f"ps_q{i}", [P, 512]) for i in range(2)]

        ident_in = sem("ident_in")
        const_in = sem("const_in")
        wattn_in = sem("wattn_in")
        x_in = sem("x_in")
        mask_in = sem("mask_in")
        consts_ready = sem("consts_ready")
        w_hi_ready = sem("w_hi_ready")
        w_lo_ready = sem("w_lo_ready")
        zeroed = sem("zeroed")
        rhs_zeroed = sem("rhs_zeroed")
        kt_mm = sem("kt_mm")
        kt_ready = sem("kt_ready")
        v_mm = sem("v_mm")
        v1_ready = sem("v1_ready")
        r1_ready = sem("r1_ready")
        v2_ready = sem("v2_ready")
        v3_ready = sem("v3_ready")
        kb0_raw_done = sem("kb0_raw_done")
        kb0_lo_done = sem("kb0_lo_done")
        kb_raw_done = sem("kb_raw_done")
        kb_hi_done = sem("kb_hi_done")
        kb_lo_done = sem("kb_lo_done")
        kb_stored = sem("kb_stored")
        vb_mm = sem("vb_mm")
        vb_done = sem("vb_done")
        vcur_ready = sem("vcur_ready")
        kmax_in = sem("kmax_in")
        kcur_in = sem("kcur_in")
        mask_ready = sem("mask_ready")
        stats_ready = sem("stats_ready")
        rstd_ready = sem("rstd_ready")
        stat_step = sem("stat_step")
        aggr_step = sem("aggr_step")
        xc_ready = sem("axc_ready")
        xn_ready = sem("xn_ready")
        xb_ready = sem("xb_ready")
        xt_filled = sem("xt_filled")
        xt_hi_ready = sem("xt_hi_ready")
        xt_lo_ready = sem("xt_lo_ready")
        q_filled = sem("q_filled")
        q_hi_ready = sem("q_hi_ready")
        q_lo_ready = sem("q_lo_ready")
        mx_filled = sem("mx_filled")
        mx_used = sem("mx_used")
        mx_hi_step = sem("mx_hi_step")
        mm_ready = sem("mm_ready")
        mt_filled = sem("mt_filled")
        mt_ready = sem("mt_ready")
        nan_step = sem("nan_step")
        nan_ready = sem("nan_ready")
        sc_filled = sem("sc_filled")
        pf_ready = sem("pf_ready")
        p_lo_ready = sem("p_lo_ready")
        pv_filled = sem("pv_filled")
        den_step = sem("den_step")
        rden_step = sem("rden_step")
        o_ready = sem("o_ready")
        ot_filled = sem("ot_filled")
        ot_hi_ready = sem("ot_hi_ready")
        ot_lo_ready = sem("ot_lo_ready")
        op_filled = sem("op_filled")
        x1_ready = sem("x1_ready")

        x_v = a["x"].rearrange("b (g p i) d -> (b g) p i d", p=P, i=TG)
        mk_v = a["mask_tok"]
        mt_v = a["mask_key"]
        Q, K, V, O = range(4)

        NCONST = 16 * 3
        NATTN = 16 * (4 + 4 + 1)

        def rows_at(g):
            return 0 if isinstance(g, int) and g == NG else g * TG

        VALUE_TILES = ((0, 3), (3, NJ))
        VALUE_PARTS = {(0, 0): (0, 1), (0, 1): (2, 3)}
        VALUE_PARTS.update({(0, j): (4 + j - 2,) for j in range(2, C * NJ)})
        VALUE_PARTS.update({(1, j): (12 + j - 6,) for j in range(6, C * NJ)})

        KEYS_AT = {(0, 1): 1, (1, 1): 2, (1, 9): 3}

        QUOTA = [-(-3 * TG * j // (C * NJ - 1)) for j in range(C * NJ)]

        block = ctx.enter_context(nc.Block())

        @block.sync
        def _(sp):
            def load_x(g):
                if g:
                    sp.wait_ge(x_in, 16 * g)
                sp.dma_start(x_res[:, g * TG:(g + 1) * TG, :], x_v[g]).then_inc(x_in, 16)

            load_x(0)
            sp.dma_start(ident[:], a["c_ident"]).then_inc(ident_in, 16)
            for i, name in enumerate(("wq", "wk", "wv", "wo")):
                sp.dma_start(w_raw[:, i], a[name].rearrange("(c p) n -> p c n", p=P)).then_inc(wattn_in, 16)
            sp.dma_start(ctx_t[:], a["ctx_t"].rearrange("(c p) n -> p c n", p=P)).then_inc(wattn_in, 16)
            sp.dma_start(bq[:], a["bq"]).then_inc(wattn_in, 16)
            sp.dma_start(bk[:], a["bk"]).then_inc(wattn_in, 16)
            sp.dma_start(bv[:], a["bv"]).then_inc(wattn_in, 16)
            sp.dma_start(bo[:], a["bo"].to_broadcast([P, D])).then_inc(wattn_in, 16)
            sp.dma_start(ksel[:], a["c_ksel"]).then_inc(const_in, 16)
            sp.dma_start(mk_raw[:], mk_v.rearrange("g p k -> p g k")).then_inc(mask_in, 16)
            sp.dma_start(mt_raw[:], mt_v.rearrange("g k t -> k g t")).then_inc(mask_in, 16)
            sp.dma_start(sel_raw, a["c_sel"]).then_inc(const_in, 16)
            sp.dma_start(vmask[:].rearrange("p j h -> p (j h)"), a["c_vmask"]).then_inc(const_in, 16)
            for g in range(1, NG):
                load_x(g)
            sp.dma_start(both.r_raw[:], a["router"].rearrange("(c p) e -> p c e", p=P)).then_inc(both.r_in, 16)
            for n in range(NRAW):
                load_network(sp, a, both, n)

            def store(b):
                sp.wait_ge(kb_lo_done, b)
                sp.dma_start(kscr[b], f32(kb_part[:]).rearrange("p h c n -> p (h c n)")).then_inc(kb_stored, 16)

            def load_kmax(b):
                sp.wait_ge(kb_stored, 16 * b)
                sp.wait_ge(mx_filled, 3 * TG * 2 * b)
                sp.dma_start(f32(kmax[:]).rearrange("p c n -> p (c n)"), kscr[b, :, 0:C * HK]).then_inc(kmax_in, 16)

            def load_kcur(b):
                sp.wait_ge(sc_filled, C * NJ * 2 * b)
                sp.dma_start(f32(kcur[:]).rearrange("p h c n -> p (h c n)"), kscr[b]).then_inc(kcur_in, 16)

            store(1)
            load_kmax(1)
            store(2)
            load_kcur(1)
            store(3)
            for b in range(2, B):
                load_kmax(b)
                load_kcur(b)

        @block.gpsimd
        def _(pool):
            g_ = nc.gpsimd
            g_.memset(ones1[:], 1.0).then_inc(zeroed, 1)
            g_.memset(pow_e[:], -0.5).then_inc(zeroed, 1)
            g_.memset(v_part[:], 0.0).then_inc(zeroed, 1)
            pool.wait_ge(zeroed, 3)
            g_.memset(v_part[:, :, 0:HEADS, 0, HD:], 1.0).then_inc(zeroed, 1)

            def norm(g):
                pool.wait_ge(stats_ready, g + 1)
                g_.tensor_tensor(rstd[:], ve[:], pow_e[:], ALU.pow).then_inc(rstd_ready, 1)

            def biased(g):
                pool.wait_ge(xn_ready, TG * (g + 1))
                for i in range(TG):
                    at = x_res[:, bass.ds(g * TG + i, 1), :].rearrange("p o d -> p (o d)")
                    g_.tensor_tensor(at, at, bo[:], ALU.add).then_inc(xb_ready, 1)

            def keys_of(b):
                pool.wait_ge(kb_hi_done, b + 1)
                if b > 1:
                    pool.wait_ge(kb_lo_done, b - 1)
                else:
                    pool.wait_ge(kb0_lo_done, 1)
                for c in range(C):
                    last = g_.tensor_tensor(kb[:, c], kt[:, c, b].unsqueeze(1).to_broadcast([P, HC, KEYS]),
                                            ksel[:].unsqueeze(2).to_broadcast([P, HC, KEYS]), ALU.mult)
                last.then_inc(kb_raw_done, 1)
                pool.wait_ge(kb_hi_done, b + 2)
                g_.tensor_tensor(kb_part[:, 1], kb[:].rearrange("p c h k -> p c (h k)"), f32(kb_part[:, 0]), ALU.subtract
                                 ).then_inc(kb_lo_done, 1)

            norm(0)
            pool.wait_ge(wattn_in, NATTN)
            biased(0)
            norm(1)
            biased(1)
            pool.wait_ge(const_in, NCONST)
            pool.wait_ge(kt_ready, C)
            keys_of(1)
            for g in (2, 3):
                norm(g)
                biased(g)
                keys_of(g)
            with pool.Fori(4, NG) as g:
                norm(g)
                biased(g)
            norm(NG)

        @block.scalar
        def _(act):
            def copy(dst, src):
                return nc.scalar.activation(dst, src, ACT.Copy)

            def normalise(g, i):
                act.wait_ge(rstd_ready, g + 1)
                if not (isinstance(g, int) and g == 0):
                    act.wait_ge(xt_filled, 2 * g)
                at = x_res[:, bass.ds(rows_at(g) + i, 1), :].rearrange("p o d -> p (o d)")
                nc.scalar.activation(xc[:, i], at, ACT.Identity, bias=negm[:, i:i + 1]).then_inc(xc_ready, 1)
                act.wait_ge(xc_ready, TG * g + i + 1)
                nc.scalar.activation(xn[:, i], xc[:, i], ACT.Copy, scale=rstd[:, i:i + 1]).then_inc(xn_ready, 1)

            def rows_high(g):
                act.wait_ge(q_filled, C * g)
                for k in range(2):
                    act.wait_ge(xt_filled, 2 * g + k + 1)
                    copy(xnt_hi[:, 2 * k:2 * k + 2], ps_t[k][:]).then_inc(xt_hi_ready, 1)

            def maxima_taken(g, u):
                act.wait_ge(mt_filled, g + 1)
                if isinstance(g, int) and g == 0:
                    act.wait_ge(rhs_zeroed, 1)
                for i in range(TG):
                    last = copy(rhs_mm[MROW:, u, i * P:(i + 1) * P],
                                ps_t[1][2 * HEADS * i:2 * HEADS * (i + 1), 0, 0])
                last.then_inc(mt_ready, 1)

            def queries_high(g, u):
                for c in range(C):
                    act.wait_ge(q_filled, C * g + c + 1)
                    nc.scalar.activation(q_hi[:, u, c], ps_q[c][:], ACT.Identity, bias=bq[:, c:c + 1]).then_inc(q_hi_ready, 1)

            act.wait_ge(zeroed, 1)
            nc.scalar.activation(warm[:], ones1[:], ACT.Exp)
            for i in range(TG):
                normalise(0, i)
            act.wait_ge(wattn_in, NATTN)
            copy(w_hi[:, 0], w_raw[:, Q]).then_inc(w_hi_ready, 1)

            def keys_high(b):
                act.wait_ge(kb_raw_done if b else kb0_raw_done, max(b, 1))
                if b >= 2:
                    act.wait_ge(kb_stored, 16 * (b - 1))
                dst = kb_part if b else kcur
                src = kb[:].rearrange("p c h k -> p c (h k)")
                if b == 0:
                    copy(kmax[:], src).then_inc(kb_hi_done, 1)
                copy(dst[:, 0], src).then_inc(kb_hi_done, 1)

            def exps(g, j):
                rows = min(P, HK - (j % NJ) * P)
                act.wait_ge(sc_filled, C * NJ * g + j + 1)
                if not (isinstance(g, int) and g == 0):
                    act.wait_ge(pv_filled, TG * g)
                nc.scalar.activation(p_hi[0:rows, j], ps_sc[j % 2][0:rows], ACT.Exp)
                if not (isinstance(g, int) and g == 0 and j < NPF):
                    act.wait_ge(p_lo_ready, C * NJ * g + (j - NPF + 1 if j >= NPF else 0))
                nc.scalar.activation(pf[0:rows, j % NPF], ps_sc[j % 2][0:rows], ACT.Exp).then_inc(pf_ready, 1)

            def heads_transposed(g):
                for k in range(2):
                    act.wait_ge(ot_filled, 2 * g + k + 1)
                    copy(ot_hi[:, 2 * k:2 * k + 2], ps_t[k][:]).then_inc(ot_hi_ready, 1)

            act.wait_ge(ident_in, 16)
            copy(ident_b[:], ident[:]).then_inc(consts_ready, 1)
            rows_high(0)
            keys_high(0)
            queries_high(0, 0)
            for i in range(TG):
                normalise(1, i)
            act.wait_ge(zeroed, 4)
            for n in range(2):
                act.wait_ge(v_mm, n + 1)
                for k in range(2):
                    last = copy(v_part[:, 2 * n + k, 0:HEADS, 0, 0:HD],
                                ps_sc[n][0:KEYS, k * D:(k + 1) * D].rearrange("p (h d) -> p h d", d=HD))
                last.then_inc(v1_ready, 1)
            rows_high(1)
            act.wait_ge(const_in, NCONST)
            copy(sel_b[:].rearrange("p c n -> p (c n)"), sel_raw[0:KEYS]).then_inc(consts_ready, 1)
            copy(sel_r[:].rearrange("p c n -> p (c n)"), sel_raw).then_inc(consts_ready, 1)
            maxima_taken(0, 0)
            queries_high(1, 1)
            for n in range(2):
                act.wait_ge(r1_ready, n + 1)
                for k in range(2):
                    last = copy(v_part[:, 2 * n + k, 0:HEADS, 1, 0:HD],
                                v_rest[:, 2 * n + k].rearrange("p (h d) -> p h d", d=HD))
                last.then_inc(v2_ready, 1)
            copy(w_hi[:, 1], w_raw[:, O]).then_inc(w_hi_ready, 1)

            def step(g, u, scores_next=True, rows_next=True, project_next=True):
                first = isinstance(g, int) and g == 0
                if scores_next and not first:
                    queries_high(g + 1, 1 - u)
                for j in range(C * NJ):
                    exps(g, j)
                    if j == 0 and not first:
                        heads_transposed(g - 1)
                    if rows_next and 3 <= j < 3 + TG:
                        normalise(g + 2, j - 3)
                    if isinstance(g, int) and (g, j) in KEYS_AT:
                        keys_high(KEYS_AT[g, j])
                if rows_next:
                    rows_high(g + 2)
                if scores_next:
                    maxima_taken(g + 1, 1 - u)

            for g in range(2):
                step(g, g)
            with act.Fori(2, NG - 3, 2) as r:
                for u in range(2):
                    step(r + u, u)
            step(NG - 2, 0, project_next=False)
            step(NG - 1, 1, False, False, False)
            heads_transposed(NG - 1)

        @block.vector
        def _(dve):
            v_ = nc.vector

            def masks(g, u):
                if not (isinstance(g, int) and g < 2):
                    dve.wait_ge(sc_filled, C * NJ * (g - 1))
                v_.tensor_scalar(mbias[:, u].rearrange("p i k -> p (i k)"),
                                 mk_raw[:, bass.ds(g, 1)].rearrange("p o k -> p (o k)"),
                                 MASKED, None, ALU.mult).then_inc(mask_ready, 1)
                v_.tensor_scalar(rhs_mm[0:KEYS, u], mt_raw[:, bass.ds(g, 1)].rearrange("p o k -> p (o k)"),
                                 MASKED, None, ALU.mult).then_inc(mask_ready, 1)

            def nans(g, u):
                v_.tensor_scalar(allmasked[:], mx[:], MASKED / 2, 3e38, ALU.is_le, ALU.mult).then_inc(nan_step, 1)
                dve.wait_ge(nan_step, g + 1)
                v_.tensor_scalar(nanfix[:, u], allmasked[:], 3e38, 0.0, ALU.mult, ALU.mult).then_inc(nan_ready, 1)

            def stats_of(g):
                if isinstance(g, int) and g == NG:
                    dve.wait_ge(x1_ready, TG)
                else:
                    dve.wait_ge(x_in, (g + 1) * 16)
                for i in range(TG):
                    v_.bn_stats(stats[:, i], x_res[:, bass.ds(rows_at(g) + i, 1), :].rearrange("p o d -> p (o d)")
                                ).then_inc(stat_step, 1)
                dve.wait_ge(stat_step, TG * (g + 1))
                v_.memset(hold[:], 0.0)
                for i in range(TG):
                    v_.bn_aggr(mv[:, i], stats[:, i]).then_inc(aggr_step, 1)
                dve.wait_ge(aggr_step, TG * (g + 1))
                v_.tensor_scalar(negm[:], mv[:, :, 0], -1.0, None, ALU.mult)
                v_.tensor_scalar(ve[:], mv[:, :, 1], EPS, None, ALU.add).then_inc(stats_ready, 1)

            def flat(ap):
                return ap.rearrange("p t c q -> p (t c q)")

            def rows_low(g, k):
                dve.wait_ge(xt_hi_ready, 2 * g + k + 1)
                v_.tensor_tensor(flat(xnt_lo[:, 2 * k:2 * k + 2]), flat(ps_t[k][:]),
                                 f32(flat(xnt_hi[:, 2 * k:2 * k + 2])), ALU.subtract).then_inc(xt_lo_ready, 1)

            def queries_low(g, u):
                for c in range(C):
                    dve.wait_ge(q_hi_ready, C * g + c + 1)
                    v_.scalar_tensor_tensor(q_lo[:, u, c], ps_q[c][:], bq[:, c:c + 1], f32(q_hi[:, u, c]), ALU.add,
                                            ALU.subtract).then_inc(q_lo_ready, 1)

            def exp_low(g, j):
                rows = min(P, HK - (j % NJ) * P)
                dve.wait_ge(pf_ready, C * NJ * g + j + 1)
                v_.tensor_tensor(p_lo[0:rows, j], pf[0:rows, j % NPF], p_hi[0:rows, j], ALU.subtract).then_inc(p_lo_ready, 1)

            def maxima(g, units):
                for n in units:
                    i, k = n // 3, n % 3
                    h0, h1 = UNITS[k]
                    dve.wait_ge(mx_filled, 3 * TG * g + n + 1)
                    v_.tensor_reduce(mx[:, i, h0:h1],
                                     ps_mx[n % 2][:, 0:(h1 - h0) * KEYS].rearrange("p (h k) -> p h k", k=KEYS),
                                     AX.X, ALU.max).then_inc(mx_used, 1)

            def maxima_parts(g, u):
                dve.wait_ge(mx_used, 3 * TG * (g + 1))
                v_.tensor_copy(mm[:, :, 0:HEADS], mx[:]).then_inc(mx_hi_step, 1)
                dve.wait_ge(mx_hi_step, g + 1)
                v_.tensor_tensor(mm[:, :, HEADS:], mx[:], f32(mm[:, :, 0:HEADS]), ALU.subtract
                                 ).then_inc(mm_ready, 1)
                nans(g, u)

            def heads(g, u, t):
                dve.wait_ge(nan_ready, g + 1)
                num = ps_q[t % 2][:, 0:HEADS * VW].rearrange("p (h v) -> p h v", v=VW)
                dve.wait_ge(pv_filled, TG * g + t + 1)
                v_.tensor_tensor(den[:, t], num[:, :, HD], nanfix[:, u, t], ALU.add).then_inc(den_step, 1)
                dve.wait_ge(den_step, TG * g + t + 1)
                v_.reciprocal(rden[:, t], den[:, t]).then_inc(rden_step, 1)
                dve.wait_ge(rden_step, TG * g + t + 1)
                v_.tensor_tensor(o[:, t].rearrange("p (h d) -> p h d", d=HD), num[:, :, 0:HD],
                                 rden[:, t].unsqueeze(2).to_broadcast([P, HEADS, HD]), ALU.mult).then_inc(o_ready, 1)

            def residual(g, t):
                dve.wait_ge(op_filled, TG * g + t + 1)
                dve.wait_ge(xb_ready, TG * (g + 1))
                at = x_res[:, bass.ds(g * TG + t, 1), :].rearrange("p o d -> p (o d)")
                v_.tensor_tensor(at, ps_q[t % 2][:, 0:D], at, ALU.add).then_inc(x1_ready, 1)

            def heads_transposed(g, k):
                dve.wait_ge(ot_hi_ready, 2 * g + k + 1)
                v_.tensor_tensor(flat(ot_lo[:, 2 * k:2 * k + 2]), flat(ps_t[k][:]),
                                 f32(flat(ot_hi[:, 2 * k:2 * k + 2])), ALU.subtract).then_inc(ot_lo_ready, 1)

            def first_keys():
                for c in range(C):
                    last = v_.tensor_tensor(kb[:, c], kt[:, c, 0].unsqueeze(1).to_broadcast([P, HC, KEYS]),
                                            ksel[:].unsqueeze(2).to_broadcast([P, HC, KEYS]), ALU.mult)
                last.then_inc(kb0_raw_done, 1)

            def first_keys_low():
                dve.wait_ge(kb_hi_done, 2)
                v_.tensor_tensor(kcur[:, 1], kb[:].rearrange("p c h k -> p c (h k)"), f32(kcur[:, 0]), ALU.subtract
                                 ).then_inc(kb0_lo_done, 1)

            def values_of(part):
                b, c, k = part // 4, part // 2 % 2, part % 2
                j0, j1 = VALUE_TILES[k]
                n = j1 - j0
                dve.wait_ge(vb_mm, part + 1)
                dst = vb[:, b - 1, c, j0:j1] if b else vcur[:, c, j0:j1]
                v_.tensor_tensor(dst.rearrange("p j h k v -> p j h (k v)"),
                                 ps_q[k][:, 0:n * NHMAX * 3 * VW].rearrange("p (j h w) -> p j h w", j=n, h=NHMAX),
                                 vmask[:, j0:j1].unsqueeze(3).to_broadcast([P, n, NHMAX, 3 * VW]), ALU.mult
                                 ).then_inc(vb_done, 1)

            v_.memset(f32(rhs_mm[64:P]), 0.0).then_inc(rhs_zeroed, 1)
            stats_of(0)
            for c in range(C):
                dve.wait_ge(kt_mm, c + 1)
                v_.tensor_scalar(kt[:, c].rearrange("p b k -> p (b k)"), ps_sc[c][:, 0:B * KEYS], bk[:, c:c + 1], None,
                                 ALU.add).then_inc(kt_ready, 1)

            def weights_low(n, i):
                dve.wait_ge(w_hi_ready, n + 1)
                v_.tensor_tensor(w_lo[:, n], w_raw[:, i], f32(w_hi[:, n]), ALU.subtract).then_inc(w_lo_ready, 1)

            weights_low(0, Q)
            dve.wait_ge(kt_ready, C)
            dve.wait_ge(const_in, NCONST)
            first_keys()
            for k in range(2):
                rows_low(0, k)
            dve.wait_ge(mask_in, 32)
            masks(0, 0)
            stats_of(1)
            queries_low(0, 0)
            maxima(0, range(4))
            first_keys_low()
            maxima(0, range(4, 8))
            for k in range(2):
                rows_low(1, k)
            maxima(0, range(8, 3 * TG))
            maxima_parts(0, 0)
            for n in range(2):
                dve.wait_ge(v1_ready, n + 1)
                for k in range(2):
                    last = v_.tensor_tensor(v_rest[:, 2 * n + k].rearrange("p (h d) -> p h d", d=HD),
                                            ps_sc[n][0:KEYS, k * D:(k + 1) * D].rearrange("p (h d) -> p h d", d=HD),
                                            v_part[:, 2 * n + k, 0:HEADS, 0, 0:HD], ALU.subtract)
                last.then_inc(r1_ready, 1)
            queries_low(1, 1)
            masks(1, 1)
            for n in range(2):
                dve.wait_ge(v2_ready, n + 1)
                for k in range(2):
                    last = v_.tensor_tensor(v_part[:, 2 * n + k, 0:HEADS, 2, 0:HD],
                                            v_rest[:, 2 * n + k].rearrange("p (h d) -> p h d", d=HD),
                                            v_part[:, 2 * n + k, 0:HEADS, 1, 0:HD], ALU.subtract)
                last.then_inc(v3_ready, 1)
            weights_low(1, O)

            def step(g, u, scores_next=True, rows_next=True, project_next=True):
                first = isinstance(g, int) and g == 0
                if rows_next:
                    stats_of(g + 2)
                if scores_next and not first:
                    queries_low(g + 1, 1 - u)
                for j in range(C * NJ):
                    if scores_next and j:
                        maxima(g + 1, range(QUOTA[j - 1], QUOTA[j]))
                    exp_low(g, j)
                    if j < 2 and not first:
                        heads_transposed(g - 1, j)
                    if not first and 3 <= j < 3 + TG:
                        residual(g - 1, j - 3)
                    if isinstance(g, int):
                        for part in VALUE_PARTS.get((g, j), ()):
                            values_of(part)
                if scores_next:
                    maxima_parts(g + 1, 1 - u)
                for t in range(TG):
                    heads(g, u, t)
                    if rows_next and t < 2:
                        rows_low(g + 2, t)
                if u == 1 and scores_next:
                    v_.tensor_copy(vcur[:].rearrange("p c j h k v -> p (c j h k v)"),
                                   vb[:, bass.ds((g - 1) // 2, 1)].rearrange("p o c j h k v -> p (o c j h k v)")
                                   ).then_inc(vcur_ready, 1)
                if project_next:
                    masks(g + 2, u)

            for g in range(2):
                step(g, g)
            with dve.Fori(2, NG - 3, 2) as r:
                for u in range(2):
                    step(r + u, u)
            step(NG - 2, 0, project_next=False)
            step(NG - 1, 1, False, False, False)
            for k in range(2):
                heads_transposed(NG - 1, k)
            for t in range(TG):
                residual(NG - 1, t)

        @block.tensor
        def _(pe):
            mm_ = nc.tensor.matmul

            def transposed(bank, rows):
                for k in range(2):
                    for c in range(C):
                        last = nc.tensor.transpose(bank[:, k, c], rows[:, k, c * P:(c + 1) * P], ident[:])
                return last

            def split_product(dst, pairs):
                todo = [(l, r) for lh, ll, rh, rl in pairs for l, r in ((lh, rh), (ll, rh), (lh, rl))]
                for n, (l, r) in enumerate(todo):
                    last = mm_(dst, l, r, start=(n == 0), stop=(n == len(todo) - 1))
                return last

            def rows_transposed(g):
                for k in range(2):
                    pe.wait_ge(xn_ready, TG * g + 2 * k + 2)
                    transposed(ps_t[k], xn[:, 2 * k:2 * k + 2]).then_inc(xt_filled, 1)

            def queries(g):
                pe.wait_ge(xt_lo_ready, 2 * g + 2)
                for c in range(C):
                    if not (isinstance(g, int) and g < 2):
                        pe.wait_ge(o_ready, TG * (g - 2) + 3 + c)
                    split_product(ps_q[c][:], [(w_hi[:, 0, k, c * P:(c + 1) * P], w_lo[:, 0, k, c * P:(c + 1) * P],
                                                xnt_hi[:, :, k, :], xnt_lo[:, :, k, :]) for k in range(C)]
                                  ).then_inc(q_filled, 1)

            def values_of(part):
                b, c, k = part // 4, part // 2 % 2, part % 2
                j0, j1 = VALUE_TILES[k]
                if part >= 2:
                    pe.wait_ge(vb_done, part - 1)
                for j in range(j0, j1):
                    at = c * HC + TILE_HEADS[j][0]
                    w = NHMAX * 3 * VW
                    last = mm_(ps_q[k][:, (j - j0) * w:(j - j0 + 1) * w], sel_b[:, c, j * P:(j + 1) * P],
                               v_part[:, b, at:at + NHMAX].rearrange("p h k v -> p (h k v)"), start=True, stop=True)
                last.then_inc(vb_mm, 1)

            pe.wait_ge(wattn_in, NATTN)
            for c in range(C):
                for k in range(C):
                    last = mm_(ps_sc[c][:, 0:B * KEYS], w_raw[:, K, k, c * P:(c + 1) * P], ctx_t[:, k],
                               start=(k == 0), stop=(k == C - 1))
                last.then_inc(kt_mm, 1)

            def values_project(b):
                dst = ps_sc[b // 2][0:KEYS, (b % 2) * D:(b % 2 + 1) * D]
                for k in range(C):
                    mm_(dst, ctx_t[:, k, b * KEYS:(b + 1) * KEYS], w_raw[:, V, k], start=(k == 0), stop=False)
                last = mm_(dst, ones1[0:1, 0:KEYS], bv[0:1, :], start=False, stop=True)
                if b % 2:
                    last.then_inc(v_mm, 1)

            def maxima(g, u, n):
                i, k = n // 3, n % 3
                h0, h1 = UNITS[k]
                bank = ps_mx[n % 2]
                mm_(bank[:, 0:(h1 - h0) * KEYS], ident_b[:],
                    mbias[:, u, i].unsqueeze(1).to_broadcast([P, h1 - h0, KEYS]), start=True, stop=True)
                for c in range(C):
                    lo, hi = max(h0, c * HC), min(h1, (c + 1) * HC)
                    if lo < hi:
                        last = mm_(bank[:, (lo - h0) * KEYS:(hi - h0) * KEYS], q_hi[:, u, c, i * P:(i + 1) * P],
                                   kmax[:, c, (lo - c * HC) * KEYS:(hi - c * HC) * KEYS],
                                   start=False, stop=True, skip_group_check=True)
                last.then_inc(mx_filled, 1)

            def maxima_begin(g):
                pe.wait_ge(q_hi_ready, C * (g + 1))
                pe.wait_ge(mask_ready, 2 * (g + 1))
                if isinstance(g, int) and g < 2:
                    pe.wait_ge(kb_hi_done, 1)
                else:
                    pe.wait_ge(kmax_in, (g // 2) * 16)

            def maxima_transposed(g):
                pe.wait_ge(mm_ready, g + 1)
                nc.tensor.transpose(ps_t[1][:, 0, 0], f32(mm[:]).rearrange("p i h -> p (i h)"), ident[:]
                                    ).then_inc(mt_filled, 1)

            def scores(g, u, n):
                c, j = divmod(n, NJ)
                rows = min(P, HK - j * P)
                dst = ps_sc[n % 2][0:rows]
                at = slice(j * P, j * P + rows)
                mm_(dst, sel_r[:, c, at], rhs_mm[:, u], start=True, stop=False)
                mm_(dst, kcur[:, 0, c, at], q_hi[:, u, c], start=False, stop=False)
                mm_(dst, kcur[:, 1, c, at], q_hi[:, u, c], start=False, stop=False)
                mm_(dst, kcur[:, 0, c, at], q_lo[:, u, c], start=False, stop=True).then_inc(sc_filled, 1)

            def values(g, t):
                if t >= 2:
                    pe.wait_ge(o_ready, TG * g + t - 1)
                for n in range(C * NJ):
                    if t == 0:
                        pe.wait_ge(p_lo_ready, C * NJ * g + n + 1)
                    c, j = divmod(n, NJ)
                    rows = min(P, HK - j * P)
                    h0, nh = TILE_HEADS[j]
                    dst = ps_q[t % 2][:, (c * HC + h0) * VW:(c * HC + h0 + nh) * VW]
                    for i, (p, part) in enumerate(((p_hi, 0), (p_hi, 1), (p_hi, 2), (p_lo, 0), (p_lo, 1))):
                        last = mm_(dst, p[0:rows, n, t * P:(t + 1) * P],
                                   vcur[0:rows, c, j, 0:nh, part, :],
                                   start=(n == 0 and i == 0), stop=True, skip_group_check=True)
                last.then_inc(pv_filled, 1)

            def heads_transposed(g, k):
                pe.wait_ge(o_ready, TG * g + 2 * k + 2)
                transposed(ps_t[k], o[:, 2 * k:2 * k + 2]).then_inc(ot_filled, 1)

            def out_projection(g, t):
                pe.wait_ge(ot_lo_ready, 2 * g + t // 2 + 1)
                if t >= 2:
                    pe.wait_ge(x1_ready, TG * g + t - 1)
                split_product(ps_q[t % 2][:, 0:D], [(ot_hi[:, t, k], ot_lo[:, t, k], w_hi[:, 1, k], w_lo[:, 1, k])
                                                    for k in range(C)]).then_inc(op_filled, 1)

            pe.wait_ge(ident_in, 16)
            rows_transposed(0)
            pe.wait_ge(zeroed, 4)
            pe.wait_ge(kt_ready, C)
            values_project(0)
            values_project(1)
            pe.wait_ge(w_lo_ready, 1)
            queries(0)
            pe.wait_ge(consts_ready, 1)
            maxima_begin(0)
            for n in range(3 * TG):
                if n >= 2:
                    pe.wait_ge(mx_used, n - 1)
                maxima(0, 0, n)
                if n in (1, 3):
                    values_project(2 + n // 2)
                if n == 5:
                    rows_transposed(1)
            pe.wait_ge(xt_lo_ready, 4)
            maxima_transposed(0)
            pe.wait_ge(q_lo_ready, C)
            queries(1)
            pe.wait_ge(consts_ready, 3)
            pe.wait_ge(rhs_zeroed, 1)
            pe.wait_ge(r1_ready, 2)

            def step(g, u, scores_next=True, rows_next=True, project_next=True):
                first = isinstance(g, int) and g == 0
                pe.wait_ge(mt_ready, g + 1)
                if not (isinstance(g, int) and g < 2):
                    pe.wait_ge(kcur_in, (g // 2) * 16)
                else:
                    pe.wait_ge(kb0_lo_done, 1)
                for n in range(C * NJ):
                    if not (first and n < 2):
                        pe.wait_ge(pf_ready, C * NJ * g + n - 1)
                    scores(g, u, n)
                    if n == 0 and not first:
                        for k in range(2):
                            heads_transposed(g - 1, k)
                    if scores_next and n:
                        if n == 1:
                            maxima_begin(g + 1)
                        for unit in range(QUOTA[n - 1], QUOTA[n]):
                            pe.wait_ge(mx_used, 3 * TG * (g + 1) + unit - 1)
                            maxima(g + 1, 1 - u, unit)
                    if isinstance(g, int) and (g, n) == (1, 2):
                        pe.wait_ge(w_lo_ready, 2)
                    if not first and 2 <= n < 2 + TG:
                        if scores_next and n == 2:
                            pe.wait_ge(q_lo_ready, C * (g + 2))
                        out_projection(g - 1, n - 2)
                    if isinstance(g, int):
                        if (g, n) == (0, 0):
                            pe.wait_ge(v3_ready, 2)
                            pe.wait_ge(q_lo_ready, 2 * C)
                        if (g, n) == (1, 6):
                            pe.wait_ge(x1_ready, TG)
                        for part in VALUE_PARTS.get((g, n), ()):
                            values_of(part)
                if rows_next:
                    rows_transposed(g + 2)
                if isinstance(g, int) and g < 2:
                    pe.wait_ge(vb_done, VALUE_PARTS[g, C * NJ - 1][-1] + 1)
                else:
                    pe.wait_ge(vcur_ready, g // 2)
                if not first:
                    pe.wait_ge(x1_ready, TG * g)
                for t in range(TG):
                    values(g, t)
                    if t == TG - 1 and scores_next:
                        if rows_next:
                            pe.wait_ge(xt_lo_ready, 2 * g + 6)
                        maxima_transposed(g + 1)
                if project_next:
                    queries(g + 2)

            for g in range(2):
                step(g, g)
            with pe.Fori(2, NG - 3, 2) as r:
                for u in range(2):
                    step(r + u, u)
            step(NG - 2, 0, project_next=False)
            step(NG - 1, 1, False, False, False)
            for k in range(2):
                heads_transposed(NG - 1, k)
            for t in range(TG):
                out_projection(NG - 1, t)


def feed_forward(nc, a, out, both):
    x_res, ident, stats, mv, negm, ve, rstd = both.x_res, both.ident, both.stats, both.mv, both.negm, both.ve, both.rstd
    pow_e, hold, xc, xn, raw, r_raw = both.pow_e, both.hold, both.xc, both.xn, both.raw, both.r_raw
    ctx = ExitStack()
    with ctx:
        def sb(name, shape, dt=F32):
            return ctx.enter_context(nc.sbuf_tensor(name, shape, dt))

        def ps(name, shape, dt=F32):
            return ctx.enter_context(nc.psum_tensor(name, shape, dt))

        def sem(name):
            return ctx.enter_context(nc.semaphore(name))

        def f32(ap):
            return ap.bitcast(F32)

        STEPS = 20
        gu_hi = sb("gu_hi", [P, C, NU, 2 * DE], F32R)
        gu_lo = sb("gu_lo", [P, C, NU, 2 * DE], F32R)
        dn_hi = sb("dn_hi", [P, NU, D], F32R)
        dn_lo = sb("dn_lo", [P, NU, D], F32R)
        r_part = sb("r_part", [P, C, 2 * E], F32R)
        x2_hi = (both.xnt_hi, sb("x2_hi", [P, TG, C, P], F32R))
        x2_lo = (both.xnt_lo, sb("x2_lo", [P, TG, C, P], F32R))
        LROWS = P // TG
        rt = sb("rt", [P, P])
        lparts = sb("lparts", [P, TG, 2 * E])
        logit = sb("logit", [P, TG, E])
        iota = sb("iota", [P, TG, E])
        work = sb("work", [P, TG, E])
        prob = sb("prob", [P, TG, E])
        one1 = sb("one1", [P, TG, E])
        one2 = sb("one2", [P, TG, E])
        coef = sb("coef", [P, 2, TG, E])
        top = sb("top", [P, TG])
        at1 = sb("at1", [P, TG])
        rsum = sb("rsum", [P, TG])
        sg = sb("sg", [P, 2, GT])
        hid = sb("hid", [P, 2, GT])
        h_hi = sb("h_hi", [P, 2, GT], F32R)
        h_lo = sb("h_lo", [P, 2, GT], F32R)

        ps_g = [ps(f"ps_g{i}", [P, GT]) for i in range(2)]
        ps_u = [ps(f"ps_u{i}", [P, GT]) for i in range(2)]
        ps_y = [ps(f"ps_y{i}", [P, 2, D]) for i in range(2)]
        ps_r = [ps(f"ps_r{i}", [P, 2, C, P]) for i in range(2)]

        w_hi_ready = sem("fw_hi_ready")
        w0_lo_ready = sem("fw0_lo_ready")
        w_lo_ready = sem("fw_lo_ready")
        r_hi_ready = sem("r_hi_ready")
        r_lo_ready = sem("r_lo_ready")
        rt_zeroed = sem("rt_zeroed")
        stat_step = sem("f_stat_step")
        aggr_step = sem("f_aggr_step")
        stats_ready = sem("f_stats_ready")
        rstd_ready = sem("f_rstd_ready")
        xc_ready = sem("xc_ready")
        xn_ready = sem("f_xn_ready")
        xt_filled = sem("f_xt_filled")
        x2_hi_ready = sem("x2_hi_ready")
        x2_lo_ready = sem("x2_lo_ready")
        rt_filled = sem("rt_filled")
        rt_ready = sem("rt_ready")
        lg_filled = sem("lg_filled")
        iota_ready = sem("iota_ready")
        route_step = sem("route_step")
        shifted = sem("shifted")
        exped = sem("exped")
        gate_filled = sem("gate_filled")
        up_filled = sem("up_filled")
        silu_ready = sem("silu_ready")
        h_ready = sem("h_ready")
        h_hi_ready = sem("h_hi_ready")
        h_lo_ready = sem("h_lo_ready")
        y_filled = sem("y_filled")
        y_used = sem("y_used")
        out_done = sem("out_done")

        out_v = out.rearrange("b (g p i) d -> (b g) p i d", p=P, i=TG)
        block = ctx.enter_context(nc.Block())

        @block.sync
        def _(sp):
            for n in range(NRAW, NU):
                if n == NRAW:
                    sp.wait_ge(w0_lo_ready, 2)
                else:
                    sp.wait_ge(w_lo_ready, 2 * (n - NRAW))
                load_network(sp, a, both, n)
            for g in range(NG):
                sp.wait_ge(y_used, 2 * (NU - 1) * (g + 1))
                sp.dma_start(out_v[g], x_res[:, g * TG:(g + 1) * TG, :]).then_inc(out_done, 16)
            sp.wait_ge(out_done, 16 * NG)

        @block.gpsimd
        def _(pool):
            g_ = nc.gpsimd
            g_.iota(iota[:], [[0, TG], [1, E]], base=-E, channel_multiplier=0,
                    allow_small_or_imprecise_dtypes=True).then_inc(iota_ready, 1)
            g_.memset(rt[:], 0.0).then_inc(rt_zeroed, 1)

            def norm(g):
                pool.wait_ge(stats_ready, g)
                g_.tensor_tensor(rstd[:], ve[:], pow_e[:], ALU.pow).then_inc(rstd_ready, 1)

            def split(n):
                pool.wait_ge(w_hi_ready, 2 * n + 2)
                g_.tensor_tensor(gu_lo[:, :, n], raw[:, n % NRAW, 0:C], f32(gu_hi[:, :, n]), ALU.subtract).then_inc(w_lo_ready, 1)
                g_.tensor_tensor(dn_lo[:, n], raw[:, n % NRAW, C], f32(dn_hi[:, n]), ALU.subtract).then_inc(w_lo_ready, 1)

            split(1)
            split(2)
            norm(1)
            for n in range(3, NU):
                split(n)
            with pool.Fori(2, NG) as g:
                norm(g)

        @block.scalar
        def _(act):
            def copy(dst, src):
                return nc.scalar.activation(dst, src, ACT.Copy)

            def split(n):
                act.wait_ge(both.w_in[n % NRAW], 48 * (n // NRAW + 1))
                copy(gu_hi[:, :, n], raw[:, n % NRAW, 0:C]).then_inc(w_hi_ready, 1)
                copy(dn_hi[:, n], raw[:, n % NRAW, C]).then_inc(w_hi_ready, 1)

            def normalise(g, tiles):
                if tiles[0] == 0:
                    act.wait_ge(rstd_ready, g)
                    if not (isinstance(g, int) and g == 1):
                        act.wait_ge(xt_filled, 2 * (g - 1))
                for i in range(*tiles):
                    at = x_res[:, bass.ds(g * TG + i, 1), :].rearrange("p o d -> p (o d)")
                    last = nc.scalar.activation(xc[:, i], at, ACT.Identity, bias=negm[:, i:i + 1])
                last.then_inc(xc_ready, 1)
                act.wait_ge(xc_ready, 2 * (g - 1) + tiles[1] // 2)
                for i in range(*tiles):
                    last = nc.scalar.activation(xn[:, i], xc[:, i], ACT.Copy, scale=rstd[:, i:i + 1])
                last.then_inc(xn_ready, 1)

            def rows_high(g, u, k):
                act.wait_ge(xt_filled, 2 * (g - 1) + k + 1)
                copy(x2_hi[u][:, 2 * k:2 * k + 2], ps_r[k][:]).then_inc(x2_hi_ready, 1)

            def logits(g):
                act.wait_ge(rt_filled, g + 1)
                for i in range(TG):
                    last = copy(rt[LROWS * i:LROWS * i + 2 * E], ps_r[0][0:2 * E, i // C, i % C])
                last.then_inc(rt_ready, 1)

            def exps(g):
                act.wait_ge(shifted, g + 1)
                nc.scalar.activation(prob[:], work[:], ACT.Exp).then_inc(exped, 1)

            def silu(n, b):
                act.wait_ge(gate_filled, n + 1)
                nc.scalar.activation(sg[:, b], ps_g[b][:], ACT.Silu).then_inc(silu_ready, 1)

            def hidden_high(n, b):
                act.wait_ge(h_ready, n + 1)
                copy(h_hi[:, b], hid[:, b]).then_inc(h_hi_ready, 1)

            def group(g, u, more):
                for m in range(NU):
                    n, b = NU * g + m, m % 2
                    if more and m == 7:
                        logits(g + 1)
                    silu(n, b)
                    hidden_high(n, b)
                    if isinstance(g, int) and g == 0 and m + 2 < NU:
                        split(m + 2)
                    if isinstance(g, int) and g == 0 and m < 2:
                        (logits, exps)[m](0)
                    if more and m in (2, 3):
                        normalise(g + 1, (2 * m - 4, 2 * m - 2))
                    if more and m in (4, 5):
                        rows_high(g + 1, 1 - u, m - 4)
                    if more and m == NU - 1:
                        exps(g + 1)

            split(0)
            act.wait_ge(both.r_in, 16)
            copy(r_part[:, :, 0:E], r_raw[:]).then_inc(r_hi_ready, 1)
            split(1)
            act.wait_ge(rt_zeroed, 1)
            group(0, 0, True)
            with act.Fori(1, NG - 2, 2) as r:
                group(r, 1, True)
                group(r + 1, 0, True)
            group(NG - 1, 1, False)

        @block.vector
        def _(dve):
            v_ = nc.vector

            def flat(ap):
                return ap.rearrange("p t c q -> p (t c q)")

            def split_first():
                dve.wait_ge(w_hi_ready, 1)
                v_.tensor_tensor(gu_lo[:, :, 0], raw[:, 0, 0:C], f32(gu_hi[:, :, 0]), ALU.subtract).then_inc(w0_lo_ready, 1)
                dve.wait_ge(w_hi_ready, 2)
                v_.tensor_tensor(dn_lo[:, 0], raw[:, 0, C], f32(dn_hi[:, 0]), ALU.subtract).then_inc(w0_lo_ready, 1)

            def row(g, i):
                return x_res[:, bass.ds(g * TG + i, 1), :].rearrange("p o d -> p (o d)")

            def stats_of(g):
                for i in range(TG):
                    v_.bn_stats(stats[:, i], row(g, i)).then_inc(stat_step, 1)
                dve.wait_ge(stat_step, TG * g)
                v_.memset(hold[:], 0.0)
                for i in range(TG):
                    v_.bn_aggr(mv[:, i], stats[:, i]).then_inc(aggr_step, 1)
                dve.wait_ge(aggr_step, TG * g)
                v_.tensor_scalar(negm[:], mv[:, :, 0], -1.0, None, ALU.mult)
                v_.tensor_scalar(ve[:], mv[:, :, 1], EPS, None, ALU.add).then_inc(stats_ready, 1)

            def rows_low(g, u, k):
                dve.wait_ge(x2_hi_ready, 2 * (g - 1) + k + 1)
                v_.tensor_tensor(flat(x2_lo[u][:, 2 * k:2 * k + 2]), flat(ps_r[k][:]),
                                 f32(flat(x2_hi[u][:, 2 * k:2 * k + 2])), ALU.subtract).then_inc(x2_lo_ready, 1)

            steps = [0]

            def link(g, ins):
                steps[0] += 1
                ins.then_inc(route_step, 1)
                dve.wait_ge(route_step, STEPS * g + steps[0])

            def spread(ap):
                return ap.unsqueeze(2).to_broadcast([P, TG, E])

            def largest(g, values, one):
                link(g, v_.tensor_reduce(top[:], values, AX.X, ALU.max))
                link(g, v_.tensor_tensor(one, values, spread(top[:]), ALU.is_equal))

            def lowest(g, one):
                link(g, v_.scalar_tensor_tensor(one, one, -float(E), iota[:], ALU.mult, ALU.add))
                link(g, v_.tensor_reduce(at1[:], one, AX.X, ALU.min))
                link(g, v_.tensor_scalar(at1[:], at1[:], -float(E) - 1.0, float(E), ALU.min, ALU.add))
                link(g, v_.tensor_tensor(one, iota[:], spread(at1[:]), ALU.is_equal))

            def route_largest(g):
                steps[0] = 0
                dve.wait_ge(lg_filled, g + 1)
                link(g, v_.tensor_copy(lparts[:], ps_r[1][:, 0, 0].rearrange("p (t e) -> p t e", e=LROWS)[:, :, 0:2 * E]))
                link(g, v_.tensor_tensor(logit[:], lparts[:, :, 0:E], lparts[:, :, E:], ALU.add))
                largest(g, logit[:], one1[:])
                v_.tensor_tensor(work[:], logit[:], spread(top[:]), ALU.subtract).then_inc(shifted, 1)

            def route_first(g):
                steps[0] = 4
                lowest(g, one1[:])

            def route_second(g):
                steps[0] = 8
                link(g, v_.scalar_tensor_tensor(one2[:], one1[:], -3e38, logit[:], ALU.mult, ALU.add))
                largest(g, one2[:], one2[:])

            def route_second_lowest(g):
                steps[0] = 11
                lowest(g, one2[:])

            def route_coef(g, u):
                steps[0] = 15
                dve.wait_ge(exped, g + 1)
                link(g, v_.tensor_reduce(rsum[:], prob[:], AX.X, ALU.add))
                link(g, v_.reciprocal(rsum[:], rsum[:]))
                link(g, v_.tensor_tensor(prob[:], prob[:], spread(rsum[:]), ALU.mult))
                link(g, v_.tensor_tensor(one1[:], one1[:], one2[:], ALU.add))
                link(g, v_.tensor_tensor(coef[:, u], one1[:], prob[:], ALU.mult))

            def hidden(n, b):
                dve.wait_ge(silu_ready, n + 1)
                dve.wait_ge(up_filled, n + 1)
                v_.tensor_tensor(hid[:, b], sg[:, b], ps_u[b][:], ALU.mult).then_inc(h_ready, 1)

            def hidden_low(n, b):
                dve.wait_ge(h_hi_ready, n + 1)
                v_.tensor_tensor(h_lo[:, b], hid[:, b], f32(h_hi[:, b]), ALU.subtract).then_inc(h_lo_ready, 1)

            def add(g, u, m):
                n = (NU - 1) * g + m - 1
                if not (isinstance(n, int) and n == 0):
                    dve.wait_ge(y_used, 2 * n)
                for k in range(2):
                    dve.wait_ge(y_filled, 2 * n + k + 1)
                    for i in range(2):
                        t = 2 * k + i
                        weight = 1.0 if ORDER[m] >= E else coef[:, u, t, ORDER[m]:ORDER[m] + 1]
                        last = v_.scalar_tensor_tensor(row(g, t), ps_y[k][:, i], weight, row(g, t), ALU.mult, ALU.add)
                    last.then_inc(y_used, 1)

            def group(g, u, more):
                first = isinstance(g, int) and g == 0
                for m in range(NU):
                    n, b = NU * g + m, m % 2
                    hidden(n, b)
                    if first and m == 3:
                        route_coef(g, u)
                    if m > 1:
                        add(g, u, m - 1)
                    elif m == 0 and not first:
                        add(g - 1, 1 - u, NU - 1)
                    hidden_low(n, b)
                    if first and m == 1:
                        route_largest(0)
                        route_first(0)
                    if first and m == 2:
                        route_second(0)
                        route_second_lowest(0)
                    if m == 0 and not first:
                        route_second(g)
                        route_second_lowest(g)
                    if m == 2 and not first:
                        route_coef(g, u)
                    if more:
                        if m == (0 if first else 1):
                            stats_of(g + 1)
                        if m in (4, 5):
                            rows_low(g + 1, 1 - u, m - 4)
                        if m == 8:
                            route_largest(g + 1)
                        if m == 9:
                            route_first(g + 1)

            split_first()
            dve.wait_ge(r_hi_ready, 1)
            v_.tensor_tensor(r_part[:, :, E:], r_raw[:], f32(r_part[:, :, 0:E]), ALU.subtract).then_inc(r_lo_ready, 1)
            dve.wait_ge(iota_ready, 1)
            group(0, 0, True)
            with dve.Fori(1, NG - 2, 2) as r:
                group(r, 1, True)
                group(r + 1, 0, True)
            group(NG - 1, 1, False)
            add(NG - 1, 1, NU - 1)

        @block.tensor
        def _(pe):
            mm_ = nc.tensor.matmul

            def transposed(g, k):
                pe.wait_ge(xn_ready, 2 * (g - 1) + k + 1)
                if k == 0:
                    pe.wait_ge(rt_ready, g)
                else:
                    pe.wait_ge(route_step, STEPS * (g - 1) + 1)
                for i in range(2):
                    for c in range(C):
                        last = nc.tensor.transpose(ps_r[k][:, i, c], xn[:, 2 * k + i, c * P:(c + 1) * P], ident[:])
                last.then_inc(xt_filled, 1)

            def logits(g, u):
                if not (isinstance(g, int) and g == 0):
                    pe.wait_ge(x2_lo_ready, 2 * g)
                dst = ps_r[0][0:2 * E].rearrange("p t c q -> p (t c q)")
                i = 0
                for k in range(C):
                    for x in (x2_hi, x2_lo):
                        last = mm_(dst, r_part[:, k], x[u][:, :, k], start=(i == 0), stop=(i == 2 * C - 1))
                        i += 1
                last.then_inc(rt_filled, 1)

            def logits_transposed(g):
                pe.wait_ge(rt_ready, g + 1)
                nc.tensor.transpose(ps_r[1][:, 0, 0], rt[:], ident[:]).then_inc(lg_filled, 1)

            def gate_up(n, u, b, m):
                if not isinstance(n, int) or n >= 2:
                    pe.wait_ge(h_ready, n - 1)
                for bank, at, filled in ((ps_g[b], 0, gate_filled), (ps_u[b], DE, up_filled)):
                    i = 0
                    for k in range(C):
                        for w, x in ((gu_hi, x2_hi), (gu_lo, x2_hi), (gu_hi, x2_lo)):
                            last = mm_(bank[:], w[:, k, m, at:at + DE], x[u][:, :, k], start=(i == 0), stop=(i == 3 * C - 1))
                            i += 1
                    last.then_inc(filled, 1)

            def down(n, g, b, m):
                pe.wait_ge(h_lo_ready, n + 1)
                for k in range(2):
                    if m != 1 and not (isinstance(g, int) and g == 0 and m == 0):
                        pe.wait_ge(y_used, 2 * ((NU - 1) * g + max(m - 1, 0) - 1) + k + 1)
                    for i in range(2):
                        at = slice((2 * k + i) * P, (2 * k + i + 1) * P)
                        for j, (h, w) in enumerate(((h_hi, dn_hi), (h_lo, dn_hi), (h_hi, dn_lo))):
                            last = mm_(ps_y[k][:, i], h[:, b, at], w[:, m], start=(m != 1 and j == 0 and (m > 0 or i == 0)),
                                       stop=(j == 2 or m < 2), skip_group_check=(m < 2))
                    if m > 0:
                        last.then_inc(y_filled, 1)

            def group(g, u, more):
                first = isinstance(g, int) and g == 0
                if not first:
                    pe.wait_ge(x2_lo_ready, 2 * g)
                for m in range(NU):
                    n, b = NU * g + m, m % 2
                    if first and m == 0:
                        pe.wait_ge(w0_lo_ready, 1)
                    elif first:
                        pe.wait_ge(w_lo_ready, 2 * m)
                    gate_up(n, u, b, m)
                    if first and m == 1:
                        pe.wait_ge(w0_lo_ready, 2)
                    if not (first and m == 0):
                        down(n - 1, g if m else g - 1, 1 - b, (m - 1) % NU)
                    if first and m == 0:
                        pe.wait_ge(r_lo_ready, 1)
                        logits(0, 0)
                    if first and m == 1:
                        logits_transposed(0)
                    if more:
                        if m in (3, 4):
                            transposed(g + 1, m - 3)
                        if m == 6:
                            logits(g + 1, 1 - u)
                        if m == 7:
                            logits_transposed(g + 1)

            group(0, 0, True)
            with pe.Fori(1, NG - 2, 2) as r:
                group(r, 1, True)
                group(r + 1, 0, True)
            group(NG - 1, 1, False)
            down(NU * NG - 1, NG - 1, (NU - 1) % 2, NU - 1)


_NAMES = {"x": "x", "wq": "L0_xattn_wq", "wk": "L0_xattn_wk", "wv": "L0_xattn_wv", "wo": "L0_xattn_wo",
          "router": "L0_ffn_router", "eg": "L0_ffn_experts_gate", "eu": "L0_ffn_experts_up",
          "ed": "L0_ffn_experts_down", "sgate": "L0_ffn_shared_gate", "sup": "L0_ffn_shared_up",
          "sdown": "L0_ffn_shared_down"}


def kernel(**inputs):
    import concourse.bacc as _bacc
    from concourse.bass_utils import run_bass_kernel_spmd as _run

    f = {k: np.ascontiguousarray(np.asarray(v)) for k, v in inputs.items()}
    arrays = {n: f[k] for n, k in _NAMES.items()}
    arrays["ctx_t"] = np.ascontiguousarray(f["ctx_1024"].transpose(2, 0, 1).reshape(D, B * KEYS))
    for n in ("bq", "bk"):
        arrays[n] = np.ascontiguousarray(f["L0_xattn_" + n].reshape(C, P).T)
    for n in ("bv", "bo"):
        arrays[n] = f["L0_xattn_" + n].reshape(1, D)
    m = f["mask_Bx1xSxS2_bk1"].reshape(NG, P, TG, KEYS)
    arrays["mask_tok"] = m.reshape(NG, P, TG * KEYS)
    arrays["mask_key"] = np.ascontiguousarray(m.transpose(0, 3, 2, 1).reshape(NG, KEYS, GT))
    arrays.update(constants())
    nc = _bacc.Bacc("TRN2", target_bir_lowering=False, num_devices=1)
    aps = {n: nc.dram_tensor(n + "_d", v.shape, mybir.dt.from_np(v.dtype), kind="ExternalInput").ap()
           for n, v in arrays.items()}
    out = nc.dram_tensor("out_d", (B, S, D), F32, kind="ExternalOutput").ap()
    kscr = nc.dram_tensor("k_blocks", (B, P, 2 * C * HK), F32, kind="Internal").ap()
    build(nc, aps, out, kscr)
    r = _run(nc, [{n + "_d": v for n, v in arrays.items()}], core_ids=[0])
    return r.results[0]["out_d"]
```
